# Optimizing a Trainium2 kernel written in Bass

```python
import numpy as np
import jax
import jax.numpy as jnp

def _softmax(x, axis=-1):
    return jax.nn.softmax(x, axis=axis)

def _gelu(x):
    return jax.nn.gelu(x, approximate=True)

def _silu(x):
    return jax.nn.silu(x)

def _sigmoid(x):
    return jax.nn.sigmoid(x)

def _layernorm(x, axis=-1, eps=1e-05):
    m = jnp.mean(x, axis=axis, keepdims=True)
    v = jnp.var(x, axis=axis, keepdims=True)
    return (x - m) / jnp.sqrt(v + eps)

def _scatter_add(tgt, idx, src, axis=0):
    return tgt.at[idx].add(src)

def _segment_sum(src, seg, n):
    return jax.ops.segment_sum(src, seg, n)
kernel_name = 'mk_prb_d1_jaxref_r4_57c1df'

def setup_inputs(seed: int=0):
    np.random.seed(seed)
    _w = jnp.asarray

    def _L0_attn_setup():
        import jax, jax.numpy as jnp
        import numpy as np
        HEADS = 16
        DIM_HEAD = 64
        B, T, C = (4, 512, 256)

        def apply_rope(x):
            d = x.shape[-1]
            seq_len = x.shape[1]
            inv_freq = 1.0 / 10000.0 ** (jnp.arange(0, d, 2, dtype=jnp.float32) / d)
            pos = jnp.arange(seq_len, dtype=jnp.float32)
            ang = pos[:, None] * inv_freq[None, :]
            sin = jnp.sin(ang)[None]
            cos = jnp.cos(ang)[None]
            x1, x2 = (x[..., 0::2], x[..., 1::2])
            rot = jnp.stack([x1 * cos - x2 * sin, x1 * sin + x2 * cos], axis=-1)
            return rot.reshape(x.shape)
        key = jax.random.key(seed)
        ks = jax.random.split(key, 6)
        inner = HEADS * DIM_HEAD
        w = 0.02
        return {'x': jax.random.normal(ks[0], (B, T, C), dtype=jnp.float32), 'Wq': jax.random.normal(ks[1], (C, inner), dtype=jnp.float32) * w, 'Wk': jax.random.normal(ks[2], (C, inner), dtype=jnp.float32) * w, 'Wv': jax.random.normal(ks[3], (C, inner), dtype=jnp.float32) * w, 'Wo': jax.random.normal(ks[4], (inner, C), dtype=jnp.float32) * w, 'bo': jnp.zeros((C,), dtype=jnp.float32)}
    _L0_attn_in = _L0_attn_setup()

    def _L0_ffn_setup():
        import jax, jax.numpy as jnp
        import numpy as np
        B, S, D, E, H, K = (64, 512, 256, 32, 1024, 8)
        key = jax.random.key(seed)
        k0, k1, k2, k3 = jax.random.split(key, 4)
        x = jax.random.normal(k0, (B, S, D), jnp.float32)
        gate_w = jax.random.normal(k1, (E, D), jnp.float32) * (1.0 / np.sqrt(D))
        gate_b = jnp.zeros((E,), jnp.float32)
        w1 = jax.random.normal(k2, (E, D + 1, H), jnp.float32) * (1.0 / np.sqrt(D + 1))
        w2 = jax.random.normal(k3, (E, H + 1, D), jnp.float32) * (1.0 / np.sqrt(H + 1))
        return {'x': x, 'gate_w': gate_w, 'gate_b': gate_b, 'w1': w1, 'w2': w2}
    _L0_ffn_in = _L0_ffn_setup()
    _d = {'L0_attn_x': _L0_attn_in['x'], 'L0_attn_Wq': _L0_attn_in['Wq'], 'L0_attn_Wk': _L0_attn_in['Wk'], 'L0_attn_Wv': _L0_attn_in['Wv'], 'L0_attn_Wo': _L0_attn_in['Wo'], 'L0_attn_bo': _L0_attn_in['bo'], 'L0_ffn_gate_w': _L0_ffn_in['gate_w'], 'L0_ffn_gate_b': _L0_ffn_in['gate_b'], 'L0_ffn_w1': _L0_ffn_in['w1'], 'L0_ffn_w2': _L0_ffn_in['w2']}
    _x0 = _d['L0_attn_x']
    _d['L0_attn_x'] = jax.random.normal(jax.random.fold_in(jax.random.key(seed), 1), (4, 1024, 256), dtype=_x0.dtype)
    del _x0
    return _d

def reference(L0_attn_x, L0_attn_Wq, L0_attn_Wk, L0_attn_Wv, L0_attn_Wo, L0_attn_bo, L0_ffn_gate_w, L0_ffn_gate_b, L0_ffn_w1, L0_ffn_w2):

    def _L0_attn_ref(x, Wq, Wk, Wv, Wo, bo):
        import jax, jax.numpy as jnp
        import numpy as np
        HEADS = 16
        DIM_HEAD = 64
        B, T, C = (4, 512, 256)

        def apply_rope(x):
            d = x.shape[-1]
            seq_len = x.shape[1]
            inv_freq = 1.0 / 10000.0 ** (jnp.arange(0, d, 2, dtype=jnp.float32) / d)
            pos = jnp.arange(seq_len, dtype=jnp.float32)
            ang = pos[:, None] * inv_freq[None, :]
            sin = jnp.sin(ang)[None]
            cos = jnp.cos(ang)[None]
            x1, x2 = (x[..., 0::2], x[..., 1::2])
            rot = jnp.stack([x1 * cos - x2 * sin, x1 * sin + x2 * cos], axis=-1)
            return rot.reshape(x.shape)
        b, t, c = x.shape
        h, d = (HEADS, DIM_HEAD)
        scale = d ** (-0.5)

        def split_heads(z):
            return z.reshape(b, t, h, d).transpose(0, 2, 1, 3).reshape(b * h, t, d)
        q = split_heads(x @ Wq)
        k = split_heads(x @ Wk)
        v = split_heads(x @ Wv)
        q = apply_rope(q)
        k = apply_rope(k)
        sim = jnp.einsum('bid,bjd->bij', q, k) * scale
        causal = jnp.tril(jnp.ones((t, t), dtype=bool))
        sim = jnp.where(causal[None], sim, -jnp.inf)
        attn = jax.nn.softmax(sim, axis=-1)
        out = jnp.einsum('bij,bjd->bid', attn, v)
        out = out.reshape(b, h, t, d).transpose(0, 2, 1, 3).reshape(b, t, h * d)
        return out @ Wo + bo

    def _L0_ffn_ref(x, gate_w, gate_b, w1, w2):
        import jax, jax.numpy as jnp
        import numpy as np
        B, S, D, E, H, K = (64, 512, 256, 32, 1024, 8)
        b, s, d = x.shape
        logits = jnp.einsum('bsd,ed->bse', x, gate_w) + gate_b
        probs = jax.nn.softmax(logits, axis=-2)
        vals_t, idx_t = jax.lax.top_k(probs.transpose(0, 2, 1), K)
        vals = vals_t.transpose(0, 2, 1)
        idx = idx_t.transpose(0, 2, 1)
        flat_idx = idx.reshape(b, K * E)
        tok = jnp.take_along_axis(x, flat_idx[:, :, None], axis=1)
        tok = tok.reshape(b, K, E, d)
        merged = jnp.einsum('bked,bke->bed', tok, vals)
        ones = jnp.ones(merged.shape[:-1] + (1,), merged.dtype)
        h = jnp.einsum('bei,eih->beh', jnp.concatenate([merged, ones], -1), w1)
        h = jax.nn.gelu(h, approximate=False)
        o = jnp.einsum('bej,ejo->beo', jnp.concatenate([h, ones], -1), w2)
        out_tok = jnp.einsum('beo,bke->bkeo', o, vals).reshape(b, K * E, d)
        out = jnp.zeros_like(x).at[jnp.arange(b)[:, None], flat_idx].add(out_tok)
        return out
    x = L0_attn_x
    xn = _layernorm(x, axis=-1)
    x = x + _L0_attn_ref(xn, L0_attn_Wq, L0_attn_Wk, L0_attn_Wv, L0_attn_Wo, L0_attn_bo) + _L0_ffn_ref(xn, L0_ffn_gate_w, L0_ffn_gate_b, L0_ffn_w1, L0_ffn_w2)
    return x

_drawn_inputs = setup_inputs


def setup_inputs(seed=0):
    import zlib

    import numpy as np

    out = dict(_drawn_inputs(seed))
    spreads = {'L0_attn_bo': (0.0, 0.1), 'L0_ffn_gate_b': (0.0, 0.1)}
    factors = {'L0_attn_Wq': 8.0, 'L0_attn_Wk': 8.0, 'L0_attn_Wv': 3.311, 'L0_attn_Wo': 3.303}
    for name, (base, spread) in spreads.items():
        noise = np.random.default_rng([zlib.crc32(name.encode()), seed]).standard_normal(out[name].shape)
        drawn = base * np.exp(spread * noise) if base else spread * noise
        out[name] = jnp.asarray(drawn.astype(out[name].dtype))
    for name, factor in factors.items():
        out[name] = (out[name] * factor).astype(out[name].dtype)
    return out
```

```python
from contextlib import ExitStack

import concourse.bass as bass
from concourse import mybir

F32 = mybir.dt.float32
F32R = mybir.dt.float32r
BF16 = mybir.dt.bfloat16
ALU = mybir.AluOpType
ACT = mybir.ActivationFunctionType
AX_X = mybir.AxisListType.X

B, T, C = 4, 1024, 256
HEADS, DH = 16, 64
INNER = HEADS * DH
E, TOPK, HID = 32, 8, 1024
P128 = 128
NT = T // P128
KT = C // P128
PAIRS = HEADS // 2
QKV = 3 * P128
BANK = 512
SCALE = DH ** -0.5
EPS = 1e-5
MASKED = -1.0e30
USED = -3.0e38
Q4 = HID // 4


def build_identity(pool, ap, sem, base):
    pool.memset(ap, 0.0).then_inc(sem, 1)
    pool.wait_ge(sem, base + 1)
    pool.affine_select(out=ap, in_=ap, compare_op=ALU.not_equal, fill=1.0, base=0,
                       pattern=[[-1, ap.shape[-1]]], channel_multiplier=1).then_inc(sem, 1)


def prepare_block(nc, x, wq, wk, wv, wo, gate_w, gate_b, xt_s, w_s, wo_s, logit_s, xn_s):
    with ExitStack() as ctx:
        def sb(name, shape, dt=F32):
            return ctx.enter_context(nc.sbuf_tensor(name, shape, dt))

        def ps(name, shape):
            return ctx.enter_context(nc.psum_tensor(name, shape, F32))

        def sem(name):
            return ctx.enter_context(nc.semaphore(name))

        ident = sb("a_ident", [P128, P128])
        wraw = sb("a_wraw", [P128, 3, KT, INNER])
        whl = sb("a_whl", [P128, PAIRS, 2, KT, QKV], F32R)
        woraw = sb("a_woraw", [P128, PAIRS, C])
        wohl = sb("a_wohl", [P128, 2, PAIRS, C], F32R)
        gw = sb("a_gw", [E, C])
        gb = sb("a_gb", [E, 1])
        gT = sb("a_gT", [P128, KT, P128])
        gThl = sb("a_gThl", [P128, 2, KT, P128], F32R)
        xin = sb("a_xin", [P128, NT, C])
        xn = sb("a_xn", [P128, NT, C])
        stats = sb("a_stats", [P128, NT, 6])
        both = sb("a_both", [P128, NT])
        gap = sb("a_gap", [P128, NT])
        gap2 = sb("a_gap2", [P128, NT])
        square = sb("a_square", [P128, NT])
        mse = sb("a_mse", [P128, NT])
        mean = sb("a_mean", [P128, NT])
        ve = sb("a_ve", [P128, NT])
        sd = sb("a_sd", [P128, NT])
        r0 = sb("a_r0", [P128, NT])
        r1 = sb("a_r1", [P128, NT])
        r2 = sb("a_r2", [P128, NT])
        r3 = sb("a_r3", [P128, NT])
        rstd = sb("a_rstd", [P128, NT])
        xThl = sb("a_xThl", [P128, 2, KT, T], F32R)
        lg = sb("a_lg", [E, T])
        pT = ps("a_pT", [P128, KT, T])
        pL = ps("a_pL", [P128, T])
        pG = ps("a_pG", [P128, BANK])

        w_loaded = sem("a_w_loaded")
        wo_loaded = sem("a_wo_loaded")
        g_loaded = sem("a_g_loaded")
        x_loaded = sem("a_x_loaded")
        ident_made = sem("a_ident_made")
        w_hi = sem("a_w_hi")
        w_lo = sem("a_w_lo")
        wo_hi = sem("a_wo_hi")
        wo_lo = sem("a_wo_lo")
        g_trans = sem("a_g_trans")
        g_zero = sem("a_g_zero")
        g_copied = sem("a_g_copied")
        g_hi = sem("a_g_hi")
        g_lo = sem("a_g_lo")
        stat_done = sem("a_stat_done")
        sqrt_done = sem("a_sqrt_done")
        xn_done = sem("a_xn_done")
        xt_done = sem("a_xt_done")
        xt_hi = sem("a_xt_hi")
        xt_lo = sem("a_xt_lo")
        logit_done = sem("a_logit_done")
        lg_done = sem("a_lg_done")
        w_stored = sem("a_w_stored")
        b_stored = sem("a_b_stored")
        STAT = 9
        STORES = 4

        block = ctx.enter_context(nc.Block())

        @block.sync
        def _(sp):
            sp.dma_start(gw[:, :], gate_w).then_inc(g_loaded, 16)
            sp.dma_start(gb[:, :], gate_b.rearrange("(e a) -> e a", a=1)).then_inc(g_loaded, 16)
            with sp.Fori(0, B) as b:
                sp.wait_ge(xn_done, b * NT)
                sp.dma_start(xin[:, :, :], x[b, :, :].rearrange("(t p) c -> p t c", p=P128)).then_inc(x_loaded, 16)
                sp.wait_ge(xn_done, (b + 1) * NT)
                sp.dma_start(xn_s[b, :, :, :], xn[:, :, :]).then_inc(b_stored, 16)
                sp.wait_ge(xt_hi, b + 1)
                sp.dma_start(xt_s[b, :, 0, :, :], xThl[:, 0, :, :].bitcast(F32)).then_inc(b_stored, 16)
                sp.wait_ge(xt_lo, b + 1)
                sp.dma_start(xt_s[b, :, 1, :, :], xThl[:, 1, :, :].bitcast(F32)).then_inc(b_stored, 16)
                sp.wait_ge(lg_done, b + 1)
                sp.dma_start(logit_s[b, :, :], lg[:, :]).then_inc(b_stored, 16)
            sp.wait_ge(b_stored, B * STORES * 16)
            sp.wait_ge(w_stored, 48)

        @block.scalar
        def _(act):
            for n, w in enumerate((wq, wk, wv)):
                act.dma_start(wraw[:, n, :, :], w.rearrange("(k p) n -> p k n", p=P128)).then_inc(w_loaded, 16)
            act.dma_start(woraw[:, :, :], wo.rearrange("(k p) n -> p k n", p=P128)).then_inc(wo_loaded, 16)
            with act.Fori(0, B) as b:
                act.wait_ge(stat_done, b * STAT + 4)
                act.activation(sd[:, :], ve[:, :], ACT.Sqrt).then_inc(sqrt_done, 1)
                for k in range(KT):
                    act.wait_ge(xt_done, b * KT + k + 1)
                    hi = act.activation(xThl[:, 0, k, :], pT[:, k, :], ACT.Copy)
                hi.then_inc(xt_hi, 1)
                act.wait_ge(logit_done, b + 1)
                act.activation(lg[:, :], pL[0:E, :], ACT.Identity, bias=gb[:, :]).then_inc(lg_done, 1)
            act.wait_ge(w_lo, 3)
            act.dma_start(w_s.rearrange("r p h k n -> p r (h k n)"),
                          whl[:, :, :, :, :].rearrange("p r h k n -> p r (h k n)").bitcast(F32)).then_inc(w_stored, 16)
            act.wait_ge(wo_lo, 1)
            act.dma_start(wo_s[:, 0, :, :], wohl[:, 0, :, :].bitcast(F32)).then_inc(w_stored, 16)
            act.dma_start(wo_s[:, 1, :, :], wohl[:, 1, :, :].bitcast(F32)).then_inc(w_stored, 16)
            act.wait_ge(w_stored, 48)

        @block.gpsimd
        def _(pool):
            build_identity(pool, ident[:, :], ident_made, 0)
            pool.memset(gT[:, :, :], 0.0).then_inc(g_zero, 1)
            pool.wait_ge(w_loaded, 48)
            for n in range(3):
                for k in range(KT):
                    last = pool.tensor_scalar(whl[:, :, 0, k, n * P128:(n + 1) * P128],
                                              wraw[:, n, k, :].rearrange("p (r c) -> p r c", c=P128),
                                              SCALE if n == 0 else 1.0, 1.0, ALU.mult, ALU.mult)
                last.then_inc(w_hi, 1)
            pool.wait_ge(wo_loaded, 16)
            pool.tensor_copy(wohl[:, 0, :, :], woraw[:, :, :]).then_inc(wo_hi, 1)

        @block.vector
        def _(dve):
            dve.wait_ge(g_trans, 1)
            dve.wait_ge(g_zero, 1)
            dve.tensor_copy(gT[:, :, 0:E], pG[:, 0:KT * E].rearrange("p (k e) -> p k e", k=KT)).then_inc(g_copied, 1)
            dve.wait_ge(g_copied, 1)
            dve.tensor_copy(gThl[:, 0, :, :], gT[:, :, :]).then_inc(g_hi, 1)
            dve.wait_ge(g_hi, 1)
            dve.tensor_tensor(gThl[:, 1, :, :], gT[:, :, :], gThl[:, 0, :, :].bitcast(F32), ALU.subtract).then_inc(g_lo, 1)
            with dve.Fori(0, B) as b:
                dve.wait_ge(x_loaded, (b + 1) * 16)
                for t in range(NT):
                    st = dve.bn_stats(stats[:, t, :], xin[:, t, :])
                st.then_inc(stat_done, 1)
                dve.wait_ge(stat_done, b * STAT + 1)
                dve.tensor_tensor(both[:, :], stats[:, :, 1], stats[:, :, 4], ALU.add)
                dve.tensor_tensor(gap[:, :], stats[:, :, 1], stats[:, :, 4], ALU.subtract)
                dve.tensor_tensor(square[:, :], stats[:, :, 2], stats[:, :, 5], ALU.add).then_inc(stat_done, 1)
                dve.wait_ge(stat_done, b * STAT + 2)
                dve.tensor_scalar(mean[:, :], both[:, :], 0.5, None, ALU.mult)
                dve.tensor_tensor(gap2[:, :], gap[:, :], gap[:, :], ALU.mult)
                dve.tensor_scalar(mse[:, :], square[:, :], 1.0 / C, EPS, ALU.mult, ALU.add).then_inc(stat_done, 1)
                dve.wait_ge(stat_done, b * STAT + 3)
                dve.scalar_tensor_tensor(ve[:, :], gap2[:, :], 0.25, mse[:, :], ALU.mult, ALU.add).then_inc(stat_done, 1)
                dve.wait_ge(sqrt_done, b + 1)
                dve.reciprocal(r0[:, :], sd[:, :]).then_inc(stat_done, 1)
                dve.wait_ge(stat_done, b * STAT + 5)
                dve.tensor_tensor(r1[:, :], r0[:, :], r0[:, :], ALU.mult).then_inc(stat_done, 1)
                dve.wait_ge(stat_done, b * STAT + 6)
                dve.tensor_tensor(r2[:, :], r1[:, :], ve[:, :], ALU.mult).then_inc(stat_done, 1)
                dve.wait_ge(stat_done, b * STAT + 7)
                dve.tensor_scalar(r3[:, :], r2[:, :], -0.5, 1.5, ALU.mult, ALU.add).then_inc(stat_done, 1)
                dve.wait_ge(stat_done, b * STAT + 8)
                dve.tensor_tensor(rstd[:, :], r3[:, :], r0[:, :], ALU.mult).then_inc(stat_done, 1)
                dve.wait_ge(stat_done, b * STAT + 9)
                dve.wait_ge(b_stored, b * STORES * 16)
                for t in range(NT):
                    dve.tensor_scalar(xn[:, t, :], xin[:, t, :], mean[:, t:t + 1], rstd[:, t:t + 1],
                                      ALU.subtract, ALU.mult).then_inc(xn_done, 1)
                for k in range(KT):
                    dve.wait_ge(xt_done, b * KT + k + 1)
                    dve.wait_ge(xt_hi, b + 1)
                    lo = dve.tensor_tensor(xThl[:, 1, k, :], pT[:, k, :], xThl[:, 0, k, :].bitcast(F32), ALU.subtract)
                lo.then_inc(xt_lo, 1)
            for n in range(3):
                dve.wait_ge(w_hi, n + 1)
                for k in range(KT):
                    last = dve.scalar_tensor_tensor(
                        whl[:, :, 1, k, n * P128:(n + 1) * P128], wraw[:, n, k, :].rearrange("p (r c) -> p r c", c=P128),
                        SCALE if n == 0 else 1.0, whl[:, :, 0, k, n * P128:(n + 1) * P128].bitcast(F32),
                        ALU.mult, ALU.subtract)
                last.then_inc(w_lo, 1)
            dve.wait_ge(wo_hi, 1)
            dve.tensor_tensor(wohl[:, 1, :, :], woraw[:, :, :], wohl[:, 0, :, :].bitcast(F32), ALU.subtract).then_inc(wo_lo, 1)

        @block.tensor
        def _(pe):
            pe.wait_ge(ident_made, 2)
            pe.wait_ge(g_loaded, 32)
            for k in range(KT):
                tr = pe.transpose(pG[:, k * E:(k + 1) * E], gw[:, k * P128:(k + 1) * P128], ident[0:E, 0:E])
            tr.then_inc(g_trans, 1)
            pe.wait_ge(g_lo, 1)
            with pe.Fori(0, B) as b:
                pe.wait_ge(xt_lo, b)
                for k in range(KT):
                    for t in range(NT):
                        pe.wait_ge(xn_done, b * NT + t + 1)
                        tr = pe.transpose(pT[:, k, t * P128:(t + 1) * P128], xn[:, t, k * P128:(k + 1) * P128], ident[:, :])
                    tr.then_inc(xt_done, 1)
                pe.wait_ge(xt_lo, b + 1)
                pe.wait_ge(lg_done, b)
                for c in range(T // BANK):
                    n = 0
                    for k in range(KT):
                        for hg, hx in ((0, 0), (0, 1), (1, 0)):
                            mm = pe.matmul(pL[:, c * BANK:(c + 1) * BANK], gThl[:, hg, k, :],
                                           xThl[:, hx, k, c * BANK:(c + 1) * BANK], start=(n == 0), stop=(n == 3 * KT - 1))
                            n += 1
                mm.then_inc(logit_done, 1)


def route_block(nc, logit_s, xn_s, wsp_s, mgt_s):
    with ExitStack() as ctx:
        def sb(name, shape, dt=F32):
            return ctx.enter_context(nc.sbuf_tensor(name, shape, dt))

        def ps(name, shape):
            return ctx.enter_context(nc.psum_tensor(name, shape, F32))

        def sem(name):
            return ctx.enter_context(nc.semaphore(name))

        ident = sb("r_ident", [P128, P128])
        L = sb("r_L", [P128, T])
        Lr = sb("r_Lr", [P128, T])
        Ex = sb("r_Ex", [P128, T])
        taken = sb("r_taken", [P128, T])
        W = sb("r_W", [P128, T])
        WT = sb("r_WT", [P128, NT, P128])
        xn = sb("r_xn", [P128, B, NT, C])
        top = sb("r_top", [P128, 8])
        nmax = sb("r_nmax", [P128, 1])
        total = sb("r_total", [P128, 1])
        rtotal = sb("r_rtotal", [P128, 1])
        mg = sb("r_mg", [P128, C])
        mgT = sb("r_mgT", [P128, KT, P128])
        pW = ps("r_pW", [P128, T])
        pM = ps("r_pM", [P128, BANK])
        pMT = ps("r_pMT", [P128, BANK])

        l_loaded = sem("r_l_loaded")
        xn_loaded = sem("r_xn_loaded")
        ident_made = sem("r_ident_made")
        dv = sem("r_dv")
        ex_done = sem("r_ex_done")
        wt_done = sem("r_wt_done")
        wt_copied = sem("r_wt_copied")
        mg_done = sem("r_mg_done")
        mgt_done = sem("r_mgt_done")
        stored = sem("r_stored")
        block = ctx.enter_context(nc.Block())

        @block.sync
        def _(sp):
            sp.dma_start(L[:, :], logit_s.rearrange("b e t -> (b e) t")).then_inc(l_loaded, 16)
            sp.dma_start(xn[:, :, :, :].rearrange("p b t c -> p b (t c)"),
                         xn_s.rearrange("b p t c -> p b (t c)")).then_inc(xn_loaded, 16)
            sp.wait_ge(dv, 6)
            sp.dma_start(wsp_s.rearrange("b e t -> (b e) t"), W[:, :]).then_inc(stored, 16)
            sp.wait_ge(dv, 8)
            sp.dma_start(mgt_s, mgT[:, :, :]).then_inc(stored, 16)
            sp.wait_ge(stored, 32)

        @block.gpsimd
        def _(pool):
            build_identity(pool, ident[:, :], ident_made, 0)

        @block.scalar
        def _(act):
            act.wait_ge(dv, 2)
            act.activation(Ex[:, :], L[:, :], ACT.Exp, bias=nmax[:, :], accum_out=total[:, :]).then_inc(ex_done, 1)
            act.wait_ge(wt_done, 1)
            act.activation(WT[:, :, :].rearrange("p t m -> p (t m)"), pW[:, :], ACT.Copy).then_inc(wt_copied, 1)

        @block.vector
        def _(dve):
            dve.wait_ge(l_loaded, 16)
            dve.max(top[:, :], L[:, :]).then_inc(dv, 1)
            dve.wait_ge(dv, 1)
            dve.tensor_scalar(nmax[:, :], top[:, 0:1], -1.0, None, ALU.mult).then_inc(dv, 1)
            dve.match_replace(out=Lr[:, :], in_to_replace=top[:, :], in_values=L[:, :], imm_value=USED).then_inc(dv, 1)
            dve.wait_ge(dv, 3)
            dve.tensor_tensor(taken[:, :], Lr[:, :], L[:, :], ALU.not_equal).then_inc(dv, 1)
            dve.wait_ge(ex_done, 1)
            dve.reciprocal(rtotal[:, :], total[:, :]).then_inc(dv, 1)
            dve.wait_ge(dv, 5)
            dve.scalar_tensor_tensor(W[:, :], Ex[:, :], rtotal[:, :], taken[:, :], ALU.mult, ALU.mult).then_inc(dv, 1)
            dve.wait_ge(mg_done, 1)
            dve.tensor_copy(mg[:, :], pM[:, 0:C]).then_inc(dv, 1)
            dve.wait_ge(mgt_done, 1)
            dve.tensor_copy(mgT[:, :, :].rearrange("p k m -> p (k m)"), pMT[:, 0:KT * P128]).then_inc(dv, 1)

        @block.tensor
        def _(pe):
            pe.wait_ge(ident_made, 2)
            pe.wait_ge(dv, 6)
            for t in range(NT):
                tr = pe.transpose(pW[:, t * P128:(t + 1) * P128], W[:, t * P128:(t + 1) * P128], ident[:, :])
            tr.then_inc(wt_done, 1)
            pe.wait_ge(wt_copied, 1)
            pe.wait_ge(xn_loaded, 16)
            for t in range(NT):
                for b in range(B):
                    mm = pe.matmul(pM[b * E:(b + 1) * E, 0:C], WT[:, t, b * E:(b + 1) * E], xn[:, b, t, :],
                                   start=(t == 0), stop=(t == NT - 1))
            mm.then_inc(mg_done, 1)
            pe.wait_ge(dv, 7)
            for k in range(KT):
                tr = pe.transpose(pMT[:, k * P128:(k + 1) * P128], mg[:, k * P128:(k + 1) * P128], ident[:, :])
            tr.then_inc(mgt_done, 1)


def experts_block(nc, w1, w2, mgt_s, o_s):
    with ExitStack() as ctx:
        def sb(name, shape, dt=F32):
            return ctx.enter_context(nc.sbuf_tensor(name, shape, dt))

        def ps(name, shape):
            return ctx.enter_context(nc.psum_tensor(name, shape, F32))

        def sem(name):
            return ctx.enter_context(nc.semaphore(name))

        ident = sb("e_ident", [P128, P128])
        fold = sb("e_fold", [P128, 32])
        mgT = sb("e_mgT", [P128, KT, B, E])
        mT = sb("e_mT", [P128, 2, KT, 32])
        w1t = sb("e_w1t", [P128, 2, KT, HID])
        w2t = sb("e_w2t", [P128, 2, 4, 2, C])
        b1 = sb("e_b1", [P128, 2, Q4])
        b2 = sb("e_b2", [B, 2, C])
        hb = sb("e_hb", [P128, 2, Q4])
        g = sb("e_g", [P128, 2, Q4])
        hT = sb("e_hT", [P128, 2, 2, P128])
        part = sb("e_part", [P128, 2, C])
        oe = sb("e_oe", [B, 2, C])
        pH = [ps(f"e_pH{i}", [P128, BANK]) for i in range(2)]
        pHT = [ps(f"e_pHT{i}", [P128, BANK]) for i in range(2)]
        pO = [ps(f"e_pO{i}", [P128, BANK]) for i in range(2)]
        pF = [ps(f"e_pF{i}", [P128, BANK]) for i in range(2)]

        m_loaded = sem("e_m_loaded")
        ident_made = sem("e_ident_made")
        fold_made = sem("e_fold_made")
        zeroed = sem("e_zeroed")
        w1_loaded = [sem(f"e_w1_loaded{i}") for i in range(2)]
        w2_loaded = [sem(f"e_w2_loaded{i}") for i in range(2)]
        b_loaded = [sem(f"e_b_loaded{i}") for i in range(2)]
        mT_done = sem("e_mT_done")
        h_done = sem("e_h_done")
        hb_done = sem("e_hb_done")
        g_done = sem("e_g_done")
        hT_done = sem("e_hT_done")
        hT_copied = sem("e_hT_copied")
        part_done = sem("e_part_done")
        part_copied = sem("e_part_copied")
        fold_done = sem("e_fold_done")
        oe_done = sem("e_oe_done")
        oe_stored = [sem(f"e_oe_stored{i}") for i in range(2)]
        block = ctx.enter_context(nc.Block())

        def load_w1(q, e, par):
            q.dma_start(w1t[:, par, :, :], w1[e, 0:C, :].rearrange("(k p) n -> p k n", p=P128)).then_inc(w1_loaded[par], 16)

        def load_w2(q, e, par):
            q.dma_start(w2t[:, par, :, :, :].rearrange("p j c n -> p j (c n)"),
                        w2[e, 0:HID, :].rearrange("(j p c) n -> p j (c n)", p=P128, c=2)).then_inc(w2_loaded[par], 16)

        def load_bias(q, e, par):
            for j in range(4):
                q.dma_start(b1[32 * j:32 * j + B, par, :],
                            w1[e, C:C + 1, j * Q4:(j + 1) * Q4].to_broadcast([B, Q4])).then_inc(b_loaded[par], 16)
            q.dma_start(b2[:, par, :], w2[e, HID:HID + 1, :].to_broadcast([B, C])).then_inc(b_loaded[par], 16)

        BIAS = 5 * 16

        @block.sync
        def _(sp):
            sp.dma_start(mgT[:, :, :, :].rearrange("p k b e -> p (k b e)"),
                         mgt_s.rearrange("p k m -> p (k m)")).then_inc(m_loaded, 16)
            for par in range(2):
                load_w1(sp, par, par)
                load_w2(sp, par, par)
            with sp.Fori(0, E // 2 - 1) as it:
                for par in range(2):
                    e = it * 2 + par
                    sp.wait_ge(h_done, e + 1)
                    load_w1(sp, e + 2, par)
                    sp.wait_ge(part_done, e + 1)
                    load_w2(sp, e + 2, par)

        @block.scalar
        def _(act):
            act.wait_ge(zeroed, 3)
            for par in range(2):
                load_bias(act, par, par)

            def steps(e, par, more):
                act.wait_ge(hb_done, e + 1)
                act.activation(g[:, par, :], hb[:, par, :], ACT.Gelu).then_inc(g_done, 1)
                act.wait_ge(part_done, e + 1)
                act.activation(part[:, par, :], pO[par][:, 0:C], ACT.Copy).then_inc(part_copied, 1)
                act.wait_ge(oe_done, e + 1)
                act.dma_start(o_s[:, e, :], oe[:, par, :]).then_inc(oe_stored[par], 16)
                if more:
                    load_bias(act, e + 2, par)

            with act.Fori(0, E // 2 - 1) as it:
                for par in range(2):
                    steps(it * 2 + par, par, True)
            for par in range(2):
                steps(E - 2 + par, par, False)
            for par in range(2):
                act.wait_ge(oe_stored[par], E // 2 * 16)

        @block.gpsimd
        def _(pool):
            pool.memset(b1[:, :, :], 0.0).then_inc(zeroed, 1)
            pool.memset(mT[:, :, :, :], 0.0).then_inc(zeroed, 1)
            pool.memset(hb[:, :, :], 0.0).then_inc(zeroed, 1)
            build_identity(pool, ident[:, :], ident_made, 0)
            pool.memset(fold[:, :], 0.0).then_inc(fold_made, 1)
            for j in range(4):
                pool.wait_ge(fold_made, j + 1)
                pool.affine_select(out=fold[:, 0:B], in_=fold[:, 0:B], compare_op=ALU.not_equal, fill=1.0,
                                   base=-32 * j, pattern=[[-1, B]], channel_multiplier=1).then_inc(fold_made, 1)

        @block.vector
        def _(dve):
            dve.wait_ge(m_loaded, 16)
            dve.wait_ge(zeroed, 3)

            def first(e, par, reuse):
                if reuse:
                    dve.wait_ge(h_done, e - 1)
                dve.tensor_copy(mT[:, par, :, 0:B], mgT[:, :, :, e]).then_inc(mT_done, 1)

            def rest(e, par, it):
                dve.wait_ge(h_done, e + 1)
                dve.wait_ge(b_loaded[par], (it + 1) * BIAS)
                dve.tensor_tensor(hb[:, par, :], pH[par][:, 0:Q4], b1[:, par, :], ALU.add).then_inc(hb_done, 1)
                dve.wait_ge(hT_done, e + 1)
                dve.tensor_copy(hT[:, par, :, :].rearrange("p c m -> p (c m)"), pHT[par][:, 0:2 * P128]).then_inc(hT_copied, 1)
                dve.wait_ge(fold_done, e + 1)
                dve.tensor_tensor(oe[:, par, :], pF[par][0:B, 0:C], b2[:, par, :], ALU.add).then_inc(oe_done, 1)

            first(0, 0, False)
            first(1, 1, False)
            rest(0, 0, 0)
            first(2, 0, True)
            rest(1, 1, 0)
            with dve.Fori(1, E // 2 - 1) as it:
                first(it * 2 + 1, 1, True)
                dve.wait_ge(oe_stored[0], it * 16)
                rest(it * 2, 0, it)
                first(it * 2 + 2, 0, True)
                dve.wait_ge(oe_stored[1], it * 16)
                rest(it * 2 + 1, 1, it)
            first(E - 1, 1, True)
            dve.wait_ge(oe_stored[0], (E // 2 - 1) * 16)
            rest(E - 2, 0, E // 2 - 1)
            dve.wait_ge(oe_stored[1], (E // 2 - 1) * 16)
            rest(E - 1, 1, E // 2 - 1)

        @block.tensor
        def _(pe):
            pe.wait_ge(ident_made, 2)
            pe.wait_ge(fold_made, 5)

            def layer1(e, par, it, reuse):
                pe.wait_ge(mT_done, e + 1)
                pe.wait_ge(w1_loaded[par], (it + 1) * 16)
                if reuse:
                    pe.wait_ge(hb_done, e - 1)
                for k in range(KT):
                    for j in range(4):
                        mm = pe.matmul(pH[par][32 * j:32 * j + 32, 0:Q4], mT[:, par, k, :],
                                       w1t[:, par, k, j * Q4:(j + 1) * Q4], start=(k == 0), stop=(k == KT - 1))
                mm.then_inc(h_done, 1)

            def layer2(e, par, it, reuse):
                pe.wait_ge(g_done, e + 1)
                if reuse:
                    pe.wait_ge(hT_copied, e - 1)
                for c in range(2):
                    tr = pe.transpose(pHT[par][:, c * P128:(c + 1) * P128], g[:, par, c::2], ident[:, :])
                tr.then_inc(hT_done, 1)
                pe.wait_ge(hT_copied, e + 1)
                pe.wait_ge(w2_loaded[par], (it + 1) * 16)
                if reuse:
                    pe.wait_ge(part_copied, e - 1)
                for c in range(2):
                    for j in range(4):
                        mm = pe.matmul(pO[par][32 * j:32 * j + 32, 0:C], hT[:, par, c, 32 * j:32 * j + 32],
                                       w2t[:, par, j, c, :], start=(c == 0), stop=(c == 1))
                mm.then_inc(part_done, 1)
                pe.wait_ge(part_copied, e + 1)
                if reuse:
                    pe.wait_ge(oe_done, e - 1)
                pe.matmul(pF[par][0:32, 0:C], fold[:, :], part[:, par, :], start=True, stop=True).then_inc(fold_done, 1)

            layer1(0, 0, 0, False)
            layer1(1, 1, 0, False)
            layer2(0, 0, 0, False)
            layer1(2, 0, 1, True)
            layer2(1, 1, 0, False)
            with pe.Fori(1, E // 2 - 1) as it:
                layer1(it * 2 + 1, 1, it, True)
                layer2(it * 2, 0, it, True)
                layer1(it * 2 + 2, 0, it + 1, True)
                layer2(it * 2 + 1, 1, it, True)
            layer1(E - 1, 1, E // 2 - 1, True)
            layer2(E - 2, 0, E // 2 - 1, True)
            layer2(E - 1, 1, E // 2 - 1, True)


def attend_block(nc, x, bo, rot_cos, rot_sin, xt_s, w_s, wo_s, wsp_s, o_s, out):
    CH = [(i + 4) // 4 for i in range(NT)]
    CHUNKS = 2 * sum(CH)
    STEPS = 2 * NT

    def chunk0(i, h):
        return 2 * sum(CH[:i]) + h * CH[i]

    with ExitStack() as ctx:
        def sb(name, shape, dt=F32):
            return ctx.enter_context(nc.sbuf_tensor(name, shape, dt))

        def ps(name, shape):
            return ctx.enter_context(nc.psum_tensor(name, shape, F32))

        def sem(name):
            return ctx.enter_context(nc.semaphore(name))

        ident = sb("t_ident", [P128, P128])
        identr = sb("t_identr", [P128, P128], F32R)
        identb = sb("t_identb", [P128, P128], BF16)
        maskb = sb("t_maskb", [P128, P128], BF16)
        cos = sb("t_cos", [P128, NT, DH])
        sin = sb("t_sin", [P128, NT, DH])
        bob = sb("t_bob", [P128, C])
        xT = sb("t_xT", [P128, 2, KT, T], F32R)
        w = sb("t_w", [P128, 2, 2, KT, QKV], F32R)
        wo = sb("t_wo", [P128, 2, PAIRS, C], F32R)
        QH = sb("t_QH", [P128, 2, 2, T], F32R)
        QL = sb("t_QL", [P128, 2, 2, T], F32R)
        KS = sb("t_KS", [P128, 2, 2, T], F32R)
        V = sb("t_V", [P128, 2, NT, P128])
        rc = sb("t_rc", [P128, 2, 2 * P128])
        rs = sb("t_rs", [P128, 2, 2 * P128])
        rq = sb("t_rq", [P128, 2, 2, 2, DH])
        rk = sb("t_rk", [P128, 2, 2, DH])
        kk = sb("t_kk", [P128, 2, 2, 2, DH], F32R)
        nmax = sb("t_nmax", [P128, 2])
        psum_row = sb("t_sum", [P128, 2, 2])
        rep = sb("t_rep", [P128, 2, 2, DH])
        Pr = sb("t_Pr", [P128, 2, T])
        PT = sb("t_PT", [P128, 2, 2, T])
        rT = sb("t_rT", [P128, P128])
        OT = sb("t_OT", [P128, PAIRS, T])
        oh = sb("t_oh", [P128, 2, PAIRS, P128], F32R)
        ol = sb("t_ol", [P128, 2, PAIRS, P128], F32R)
        wsp = sb("t_wsp", [E, T])
        oe = sb("t_oe", [E, C])
        xin = sb("t_xin", [P128, 2, C])
        xb = sb("t_xb", [P128, 2, C])
        y = sb("t_y", [P128, 2, C])
        pS = [ps(f"t_pS{i}", [P128, T]) for i in range(2)]
        pT = [ps(f"t_pT{i}", [P128, BANK]) for i in range(2)]
        pO = ps("t_pO", [P128, BANK])
        pP = ps("t_pP", [P128, BANK])

        table_loaded = sem("t_table_loaded")
        wo_loaded = sem("t_wo_loaded")
        bo_loaded = sem("t_bo_loaded")
        const_made = sem("t_const_made")
        identr_made = sem("t_identr_made")
        xt_loaded = sem("t_xt_loaded")
        w_loaded = [sem(f"t_w_loaded{i}") for i in range(2)]
        moe_loaded = sem("t_moe_loaded")
        x_loaded = [sem(f"t_x_loaded{i}") for i in range(2)]
        proj_done = sem("t_proj_done")
        rope_done = sem("t_rope_done")
        rk_done = sem("t_rk_done")
        kh_done = sem("t_kh_done")
        rot_done = sem("t_rot_done")
        stackT_done = sem("t_stackT_done")
        stack_hi = sem("t_stack_hi")
        stack_lo = sem("t_stack_lo")
        s_done = sem("t_s_done")
        max_done = sem("t_max_done")
        exp_done = sem("t_exp_done")
        t_done = sem("t_t_done")
        evac_done = sem("t_evac_done")
        rep_done = sem("t_rep_done")
        pv_done = sem("t_pv_done")
        rt_copied = sem("t_rt_copied")
        o_done = sem("t_o_done")
        oh_done = sem("t_oh_done")
        ol_done = sem("t_ol_done")
        xb_done = sem("t_xb_done")
        y_mm = sem("t_y_mm")
        y_done = sem("t_y_done")
        y_stored = [sem(f"t_y_stored{i}") for i in range(2)]
        block = ctx.enter_context(nc.Block())

        def pairs(engine, b, attend, prologue, epilogue):
            loads = b * (PAIRS // 2) + 1
            prologue()
            attend(b * PAIRS, 0, 0, True, False, loads)
            with engine.Fori(0, PAIRS // 2 - 1) as g:
                attend(b * PAIRS + g * 2 + 1, g * 2 + 1, 1, False, False, loads + g + 1)
                attend(b * PAIRS + g * 2 + 2, g * 2 + 2, 0, False, False, loads + g + 1)
            attend(b * PAIRS + PAIRS - 1, PAIRS - 1, 1, False, True, loads)
            epilogue()

        @block.sync
        def _(sp):
            sp.dma_start(cos[:, :, :], rot_cos.rearrange("(t p) d -> p t d", p=P128)).then_inc(table_loaded, 16)
            sp.dma_start(sin[:, :, :], rot_sin.rearrange("(t p) d -> p t d", p=P128)).then_inc(table_loaded, 16)
            with sp.Fori(0, B) as b:
                sp.wait_ge(proj_done, b * PAIRS * NT)
                sp.dma_start(xT[:, :, :, :].bitcast(F32), xt_s[b, :, :, :, :]).then_inc(xt_loaded, 16)
                for p in range(2):
                    sp.dma_start(w[:, p, :, :, :].bitcast(F32), w_s[p, :, :, :, :]).then_inc(w_loaded[p], 16)
                with sp.Fori(0, PAIRS // 2 - 1) as g:
                    for par in range(2):
                        sp.wait_ge(proj_done, (b * PAIRS + g * 2 + par + 1) * NT)
                        sp.dma_start(w[:, par, :, :, :].bitcast(F32), w_s[g * 2 + 2 + par, :, :, :, :]).then_inc(w_loaded[par], 16)

        @block.gpsimd
        def _(pool):
            build_identity(pool, ident[:, :], const_made, 0)
            pool.memset(maskb[:, :], 0.0).then_inc(const_made, 1)
            pool.wait_ge(const_made, 3)
            pool.affine_select(out=maskb[:, :], in_=maskb[:, :], compare_op=ALU.is_ge, fill=MASKED, base=0,
                               pattern=[[-1, P128]], channel_multiplier=1).then_inc(const_made, 1)
            pool.tensor_copy(identr[:, :], ident[:, :]).then_inc(identr_made, 1)
            pool.tensor_copy(identb[:, :], ident[:, :]).then_inc(identr_made, 1)

            def rotate(TI, u):
                pool.wait_ge(rope_done, TI + 1)
                cq = rc[:, u, 0:P128].rearrange("p (h d) -> p h d", h=2)
                sq = rs[:, u, 0:P128].rearrange("p (h d) -> p h d", h=2)
                ck = rc[:, u, P128:].rearrange("p (h d) -> p h d", h=2)
                sk = rs[:, u, P128:].rearrange("p (h d) -> p h d", h=2)
                pool.tensor_tensor(rk[:, u, :, :], ck, sk, ALU.add).then_inc(rk_done, 1)
                pool.tensor_tensor(rq[:, u, :, 0, :], cq, sq, ALU.add)
                pool.wait_ge(rk_done, TI + 1)
                pool.tensor_tensor(rq[:, u, :, 1, :], cq, sq, ALU.add)
                pool.tensor_copy(kk[:, u, :, 0, :], rk[:, u, :, :]).then_inc(kh_done, 1)
                pool.wait_ge(kh_done, TI + 1)
                pool.tensor_tensor(kk[:, u, :, 1, :], rk[:, u, :, :], kk[:, u, :, 0, :].bitcast(F32), ALU.subtract).then_inc(rot_done, 1)

            def prologue(b):
                for t in range(NT):
                    if t >= 2:
                        pool.wait_ge(stackT_done, b * PAIRS * NT + t - 1)
                    rotate(b * PAIRS * NT + t, t % 2)

            def attend(P, p, par, first, last, loads):
                if last:
                    return
                for t in range(NT):
                    TI = (P + 1) * NT + t
                    pool.wait_ge(stackT_done, TI - 1)
                    rotate(TI, t % 2)

            def epilogue(b):
                for t in range(NT):
                    u = t % 2
                    pool.wait_ge(x_loaded[u], (b * (NT // 2) + t // 2 + 1) * 16)
                    if t >= 2:
                        pool.wait_ge(y_done, b * NT + t - 1)
                    pool.tensor_tensor(xb[:, u, :], xin[:, u, :], bob[:, :], ALU.add).then_inc(xb_done, 1)

            pool.dma_start(bob[:, :], bo.rearrange("(a n) -> a n", a=1).to_broadcast([P128, C])).then_inc(bo_loaded, 16)
            pool.wait_ge(bo_loaded, 16)
            with pool.Fori(0, B) as b:
                pairs(pool, b, attend, lambda: prologue(b), lambda: epilogue(b))

        @block.scalar
        def _(act):
            act.dma_start(wo[:, :, :, :].bitcast(F32), wo_s).then_inc(wo_loaded, 16)

            def exp(SI, i, h):
                s = (2 * i + h) % 2
                act.wait_ge(max_done, SI + 1)
                act.activation(Pr[:, s, 0:(i + 1) * P128], pS[s][:, 0:(i + 1) * P128], ACT.Exp, bias=nmax[:, s:s + 1],
                               accum_out=psum_row[:, i % 2, h:h + 1]).then_inc(exp_done, 1)

            def evac(P, i, h):
                for c in range(CH[i]):
                    n = chunk0(i, h) + c
                    lo, hi = c * BANK, min((c + 1) * BANK, (i + 1) * P128)
                    act.wait_ge(t_done, P * CHUNKS + n + 1)
                    act.activation(PT[:, i % 2, h, lo:hi], pT[n % 2][:, 0:hi - lo], ACT.Copy).then_inc(evac_done, 1)

            def stack(TI, t, par):
                act.wait_ge(stackT_done, TI + 1)
                act.activation(KS[:, par, :, t * P128:(t + 1) * P128],
                               pP[:, 2 * P128:].rearrange("p (h n) -> p h n", h=2), ACT.Copy)
                act.activation(QH[:, par, :, t * P128:(t + 1) * P128],
                               pP[:, 0:2 * P128].rearrange("p (h n) -> p h n", h=2), ACT.Copy).then_inc(stack_hi, 1)

            def prologue(b):
                for t in range(NT - 1):
                    stack(b * PAIRS * NT + t, t, 0)
                exp(b * PAIRS * STEPS, 0, 0)

            def attend(P, p, par, first, last, loads):
                for i in range(NT):
                    exp(P * STEPS + 2 * i + 1, i, 1)
                    if i >= 2:
                        act.wait_ge(pv_done, P * NT + i - 1)
                    elif not first:
                        act.wait_ge(pv_done, P * NT + i - 1)
                    evac(P, i, 0)
                    if i + 1 < NT:
                        exp(P * STEPS + 2 * i + 2, i + 1, 0)
                    elif not last:
                        exp(P * STEPS + STEPS, 0, 0)
                    if i == 0:
                        stack(P * NT + NT - 1, NT - 1, par)
                    elif not last:
                        stack((P + 1) * NT + i - 1, i - 1, 1 - par)
                    evac(P, i, 1)

            def epilogue(b):
                act.dma_start(wsp[:, :], wsp_s[b, :, :]).then_inc(moe_loaded, 16)
                act.dma_start(oe[:, :], o_s[b, :, :]).then_inc(moe_loaded, 16)

                def load_x(t):
                    act.dma_start(xin[:, t % 2, :], x[b, t * P128:(t + 1) * P128, :]).then_inc(x_loaded[t % 2], 16)

                load_x(0)
                load_x(1)
                act.wait_ge(o_done, (b + 1) * PAIRS * NT)

                def rounded(t):
                    if t >= 2:
                        act.wait_ge(y_mm, b * NT + t - 1)
                    act.activation(oh[:, t % 2, :, :], OT[:, :, t * P128:(t + 1) * P128], ACT.Copy).then_inc(oh_done, 1)

                rounded(0)
                for t in range(NT):
                    u = t % 2
                    if t + 1 < NT:
                        rounded(t + 1)
                    act.wait_ge(y_done, b * NT + t + 1)
                    act.dma_start(out[b, t * P128:(t + 1) * P128, :], y[:, u, :]).then_inc(y_stored[u], 16)
                    if t + 2 < NT:
                        act.wait_ge(xb_done, b * NT + t + 1)
                        load_x(t + 2)

            with act.Fori(0, B) as b:
                pairs(act, b, attend, lambda: prologue(b), lambda: epilogue(b))
            for u in range(2):
                act.wait_ge(y_stored[u], B * NT // 2 * 16)

        @block.vector
        def _(dve):
            dve.wait_ge(table_loaded, 32)

            def rope(TI, t, par):
                u = t % 2
                dve.wait_ge(proj_done, TI + 1)
                q2 = pP[:, 0:2 * P128]
                four = [P128, 4, DH]
                dve.tensor_tensor(rc[:, u, :].rearrange("p (g d) -> p g d", d=DH), q2.rearrange("p (g d) -> p g d", d=DH),
                                  cos[:, t, :].unsqueeze(1).to_broadcast(four), ALU.mult)
                for o in range(2):
                    dve.tensor_tensor(rs[:, u, :].rearrange("p (g d o) -> p g d o", d=DH // 2, o=2)[:, :, :, o],
                                      q2.rearrange("p (g d o) -> p g d o", d=DH // 2, o=2)[:, :, :, 1 - o],
                                      sin[:, t, o::2].unsqueeze(1).to_broadcast([P128, 4, DH // 2]), ALU.mult)
                dve.tensor_copy(V[:, par, t, :], pP[:, 2 * P128:QKV]).then_inc(rope_done, 1)

            def stack(TI, t, par):
                dve.wait_ge(stack_hi, TI + 1)
                dve.tensor_tensor(QL[:, par, :, t * P128:(t + 1) * P128], pP[:, 0:2 * P128].rearrange("p (h n) -> p h n", h=2),
                                  QH[:, par, :, t * P128:(t + 1) * P128].bitcast(F32), ALU.subtract).then_inc(stack_lo, 1)

            def row_max(SI, i, h):
                s = (2 * i + h) % 2
                dve.wait_ge(s_done, SI + 1)
                dve.tensor_reduce(nmax[:, s:s + 1], pS[s][:, 0:(i + 1) * P128], AX_X, ALU.max, negate=True).then_inc(max_done, 1)

            def reciprocals(OI, SI, i):
                dve.wait_ge(exp_done, SI + 1)
                dve.reciprocal(rep[:, i % 2, :, :], psum_row[:, i % 2, :].unsqueeze(2).to_broadcast([P128, 2, DH])).then_inc(rep_done, 1)

            def values(OI, p, i):
                dve.wait_ge(pv_done, OI + 1)
                dve.tensor_copy(rT[:, :], pO[:, P128:2 * P128]).then_inc(rt_copied, 1)
                dve.wait_ge(rt_copied, OI + 1)
                dve.tensor_tensor(OT[:, p, i * P128:(i + 1) * P128], pO[:, 0:P128], rT[:, :], ALU.mult).then_inc(o_done, 1)

            def prologue(b):
                for t in range(NT):
                    if t >= 2:
                        dve.wait_ge(rot_done, b * PAIRS * NT + t - 1)
                    rope(b * PAIRS * NT + t, t, 0)
                    if t >= 1:
                        stack(b * PAIRS * NT + t - 1, t - 1, 0)
                row_max(b * PAIRS * STEPS, 0, 0)

            def attend(P, p, par, first, last, loads):
                for i in range(NT):
                    if i > 0:
                        reciprocals(P * NT + i - 1, P * STEPS + 2 * i - 1, i - 1)
                    elif not first:
                        reciprocals(P * NT - 1, P * STEPS - 1, NT - 1)
                    row_max(P * STEPS + 2 * i + 1, i, 1)
                    if i == 0 and not first:
                        values(P * NT - 1, p - 1, NT - 1)
                    if not last:
                        dve.wait_ge(rot_done, (P + 1) * NT + i - 1)
                        rope((P + 1) * NT + i, i, 1 - par)
                    if i > 0:
                        values(P * NT + i - 1, p, i - 1)
                    if i + 1 < NT:
                        row_max(P * STEPS + 2 * i + 2, i + 1, 0)
                    elif not last:
                        row_max(P * STEPS + STEPS, 0, 0)
                    if i == 0:
                        stack(P * NT + NT - 1, NT - 1, par)
                    elif not last:
                        stack((P + 1) * NT + i - 1, i - 1, 1 - par)

            def epilogue(b):
                LP = (b + 1) * PAIRS - 1
                reciprocals(LP * NT + NT - 1, LP * STEPS + STEPS - 1, NT - 1)
                values(LP * NT + NT - 1, PAIRS - 1, NT - 1)

                def rest(t):
                    u = t % 2
                    dve.wait_ge(oh_done, b * NT + t + 1)
                    if t >= 2:
                        dve.wait_ge(y_mm, b * NT + t - 1)
                    dve.tensor_tensor(ol[:, u, :, :], OT[:, :, t * P128:(t + 1) * P128], oh[:, u, :, :].bitcast(F32),
                                      ALU.subtract).then_inc(ol_done, 1)

                rest(0)
                for t in range(NT):
                    u = t % 2
                    if t + 1 < NT:
                        rest(t + 1)
                    dve.wait_ge(y_mm, b * NT + t + 1)
                    dve.wait_ge(xb_done, b * NT + t + 1)
                    dve.wait_ge(y_stored[u], (b * (NT // 2) + t // 2) * 16)
                    dve.tensor_tensor(y[:, u, :], pT[u][:, 0:C], xb[:, u, :], ALU.add).then_inc(y_done, 1)

            with dve.Fori(0, B) as b:
                pairs(dve, b, attend, lambda: prologue(b), lambda: epilogue(b))

        @block.tensor
        def _(pe):
            pe.wait_ge(const_made, 4)
            pe.wait_ge(identr_made, 2)
            pe.wait_ge(wo_loaded, 16)

            def project(TI, t, par):
                n = 0
                for k in range(KT):
                    for hx, hw in ((0, 0), (0, 1), (1, 0)):
                        mm = pe.matmul(pP[:, 0:QKV], xT[:, hx, k, t * P128:(t + 1) * P128], w[:, par, hw, k, :],
                                       start=(n == 0), stop=(n == 3 * KT - 1))
                        n += 1
                mm.then_inc(proj_done, 1)

            def stack(TI, t, more):
                u = t % 2
                pe.wait_ge(rope_done, TI + 2 if more else TI + 1)
                pe.wait_ge(rot_done, TI + 1)
                for h in range(2):
                    pe.transpose(pP[:, h * P128:(h + 1) * P128], rq[:, u, h, :, :].rearrange("p a d -> p (a d)"), ident[:, :])
                for h in range(2):
                    mm = pe.matmul(pP[:, (2 + h) * P128:(3 + h) * P128], kk[:, u, h, :, :].rearrange("p a d -> p (a d)"),
                                   identr[:, :], start=True, stop=True)
                mm.then_inc(stackT_done, 1)

            def scores(TI, SI, i, h, par, fresh):
                s = (2 * i + h) % 2
                pe.wait_ge(stack_lo, TI + 1)
                if not fresh:
                    pe.wait_ge(exp_done, SI - 1)
                width = (i + 1) * P128
                q = slice(i * P128, (i + 1) * P128)
                for c0 in range(0, width, BANK):
                    c1 = min(c0 + BANK, width)
                    diag = c1 == width
                    pe.matmul(pS[s][:, c0:c1], QH[:, par, h, q], KS[:, par, h, c0:c1], start=True, stop=False)
                    mm = pe.matmul(pS[s][:, c0:c1], QL[:, par, h, q], KS[:, par, h, c0:c1], start=False, stop=not diag)
                mm = pe.matmul(pS[s][:, width - P128:width], identb[:, :], maskb[:, :], start=False, stop=True)
                mm.then_inc(s_done, 1)

            def transposes(P, SI, i, h, lag):
                s = (2 * i + h) % 2
                pe.wait_ge(exp_done, SI + 1)
                for c in range(CH[i]):
                    n = chunk0(i, h) + c
                    if lag or n >= 2:
                        pe.wait_ge(evac_done, P * CHUNKS + n - 1)
                    for j in range(4 * c, min(4 * c + 4, i + 1)):
                        tr = pe.transpose(pT[n % 2][:, (j - 4 * c) * P128:(j - 4 * c + 1) * P128],
                                          Pr[:, s, j * P128:(j + 1) * P128], ident[:, :])
                    tr.then_inc(t_done, 1)

            def values(P, OI, i, par):
                pe.wait_ge(rep_done, OI + 1)
                pe.wait_ge(o_done, OI)
                pe.transpose(pO[:, P128:2 * P128], rep[:, i % 2, :, :].rearrange("p h d -> p (h d)"), ident[:, :])
                pe.wait_ge(evac_done, P * CHUNKS + chunk0(i, 1) + CH[i])
                for j in range(i + 1):
                    for h in range(2):
                        mm = pe.matmul(pO[h * DH:(h + 1) * DH, 0:P128], V[:, par, j, h * DH:(h + 1) * DH],
                                       PT[:, i % 2, h, j * P128:(j + 1) * P128], start=(j == 0), stop=(j == i))
                mm.then_inc(pv_done, 1)

            def prologue(b):
                pe.wait_ge(xt_loaded, (b + 1) * 16)
                pe.wait_ge(w_loaded[0], b * (PAIRS // 2) * 16 + 16)
                for t in range(NT):
                    TI = b * PAIRS * NT + t
                    if t == 1:
                        pe.wait_ge(rope_done, TI)
                    elif t >= 2:
                        pe.wait_ge(stack_lo, TI - 1)
                    project(TI, t, 0)
                    if t >= 1:
                        stack(TI - 1, t - 1, True)
                scores(b * PAIRS * NT, b * PAIRS * STEPS, 0, 0, 0, True)

            def attend(P, p, par, first, last, loads):
                if not last:
                    pe.wait_ge(w_loaded[1 - par], loads * 16)
                for i in range(NT):
                    SI = P * STEPS + 2 * i
                    scores(P * NT + i, SI + 1, i, 1, par, first and i == 0)
                    if not last:
                        TI = (P + 1) * NT + i
                        pe.wait_ge(stack_lo, TI - 1)
                        project(TI, i, 1 - par)
                    transposes(P, SI, i, 0, not first)
                    if i > 0:
                        values(P, P * NT + i - 1, i - 1, par)
                    elif not first:
                        values(P - 1, P * NT - 1, NT - 1, 1 - par)
                    if i + 1 < NT:
                        scores(P * NT + i + 1, SI + 2, i + 1, 0, par, False)
                    elif not last:
                        scores((P + 1) * NT, SI + 2, 0, 0, 1 - par, False)
                    if i == 0:
                        stack(P * NT + NT - 1, NT - 1, not last)
                    elif not last:
                        stack((P + 1) * NT + i - 1, i - 1, True)
                    transposes(P, SI + 1, i, 1, not first)

            def epilogue(b):
                LP = (b + 1) * PAIRS - 1
                values(LP, LP * NT + NT - 1, NT - 1, 1)
                pe.wait_ge(moe_loaded, (b + 1) * 32)
                for t in range(NT):
                    u = t % 2
                    if t == 0:
                        pe.wait_ge(evac_done, (b + 1) * PAIRS * CHUNKS)
                    if t >= 2:
                        pe.wait_ge(y_done, b * NT + t - 1)
                    pe.matmul(pT[u][:, 0:C], wsp[:, t * P128:(t + 1) * P128], oe[:, :], start=True, stop=False)
                    pe.wait_ge(ol_done, b * NT + t + 1)
                    n = 0
                    for k in range(PAIRS):
                        for o, hw in ((oh, 0), (oh, 1), (ol, 0)):
                            n += 1
                            mm = pe.matmul(pT[u][:, 0:C], o[:, u, k, :], wo[:, hw, k, :], start=False, stop=(n == 3 * PAIRS))
                    mm.then_inc(y_mm, 1)
                pe.wait_ge(y_done, (b + 1) * NT)

            with pe.Fori(0, B) as b:
                pairs(pe, b, attend, lambda: prologue(b), lambda: epilogue(b))


def build(nc, x, wq, wk, wv, wo, bo, gate_w, gate_b, w1, w2, rot_cos, rot_sin, out):
    def dram(name, shape):
        return nc.dram_tensor(name, shape, F32, kind="Internal").ap()

    xt_s = dram("xt_s", (B, P128, 2, KT, T))
    xn_s = dram("xn_s", (B, P128, NT, C))
    w_s = dram("w_s", (PAIRS, P128, 2, KT, QKV))
    wo_s = dram("wo_s", (P128, 2, PAIRS, C))
    logit_s = dram("logit_s", (B, E, T))
    wsp_s = dram("wsp_s", (B, E, T))
    mgt_s = dram("mgt_s", (P128, KT, P128))
    o_s = dram("o_s", (B, E, C))
    prepare_block(nc, x, wq, wk, wv, wo, gate_w, gate_b, xt_s, w_s, wo_s, logit_s, xn_s)
    route_block(nc, logit_s, xn_s, wsp_s, mgt_s)
    experts_block(nc, w1, w2, mgt_s, o_s)
    attend_block(nc, x, bo, rot_cos, rot_sin, xt_s, w_s, wo_s, wsp_s, o_s, out)


_INS = ["L0_attn_x", "L0_attn_Wq", "L0_attn_Wk", "L0_attn_Wv", "L0_attn_Wo", "L0_attn_bo",
        "L0_ffn_gate_w", "L0_ffn_gate_b", "L0_ffn_w1", "L0_ffn_w2"]


def rotation_tables():
    import numpy as np
    inv = (1.0 / 10000.0 ** (np.arange(0, DH, 2, dtype=np.float32) / np.float32(DH))).astype(np.float32)
    ang = (np.arange(T, dtype=np.float32)[:, None] * inv[None, :]).astype(np.float32)
    cos = np.repeat(np.cos(ang), 2, axis=1)
    sin = np.stack([-np.sin(ang), np.sin(ang)], axis=-1).reshape(T, DH)
    return np.ascontiguousarray(cos, dtype=np.float32), np.ascontiguousarray(sin, dtype=np.float32)


def kernel(**inputs):
    import numpy as _np
    import concourse.bacc as _bacc
    from concourse import mybir as _mybir
    from concourse.bass_utils import run_bass_kernel_spmd as _run

    nc = _bacc.Bacc("TRN2", target_bir_lowering=False, num_devices=1)
    cos, sin = rotation_tables()
    arrays, args = {}, []
    for name, a in [(n, inputs[n]) for n in _INS] + [("rot_cos", cos), ("rot_sin", sin)]:
        a = _np.ascontiguousarray(a)
        arrays[f"in_{name}"] = a
        args.append(nc.dram_tensor(f"in_{name}", a.shape, _mybir.dt.from_np(a.dtype), kind="ExternalInput").ap())
    args.append(nc.dram_tensor("out_0", (B, T, C), F32, kind="ExternalOutput").ap())
    build(nc, *args)
    r = _run(nc, [arrays], core_ids=[0])
    return r.results[0]["out_0"]
```

```python
from contextlib import ExitStack

import concourse.bass as bass
from concourse import mybir

F32 = mybir.dt.float32
F32R = mybir.dt.float32r
BF16 = mybir.dt.bfloat16
ALU = mybir.AluOpType
ACT = mybir.ActivationFunctionType
AX_X = mybir.AxisListType.X

B, T, C = 4, 1024, 256
HEADS, DH = 16, 64
INNER = HEADS * DH
E, TOPK, HID = 32, 8, 1024
P128 = 128
NT = T // P128
KT = C // P128
PAIRS = HEADS // 2
QKV = 3 * P128
BANK = 512
SCALE = DH ** -0.5
EPS = 1e-5
MASKED = -1.0e30
USED = -3.0e38
Q4 = HID // 4


def build_identity(pool, ap, sem, base):
    pool.memset(ap, 0.0).then_inc(sem, 1)
    pool.wait_ge(sem, base + 1)
    pool.affine_select(out=ap, in_=ap, compare_op=ALU.not_equal, fill=1.0, base=0,
                       pattern=[[-1, ap.shape[-1]]], channel_multiplier=1).then_inc(sem, 1)


def prepare_block(nc, x, wq, wk, wv, wo, gate_w, gate_b, xt_s, w_s, wo_s, logit_s, xn_s):
    with ExitStack() as ctx:
        def sb(name, shape, dt=F32):
            return ctx.enter_context(nc.sbuf_tensor(name, shape, dt))

        def ps(name, shape):
            return ctx.enter_context(nc.psum_tensor(name, shape, F32))

        def sem(name):
            return ctx.enter_context(nc.semaphore(name))

        ident = sb("a_ident", [P128, P128])
        wraw = sb("a_wraw", [P128, 3, KT, INNER])
        whl = sb("a_whl", [P128, PAIRS, 2, KT, QKV], F32R)
        woraw = sb("a_woraw", [P128, PAIRS, C])
        wohl = sb("a_wohl", [P128, 2, PAIRS, C], F32R)
        gw = sb("a_gw", [E, C])
        gb = sb("a_gb", [E, 1])
        gT = sb("a_gT", [P128, KT, P128])
        gThl = sb("a_gThl", [P128, 2, KT, P128], F32R)
        xin = sb("a_xin", [P128, NT, C])
        xn = sb("a_xn", [P128, NT, C])
        stats = sb("a_stats", [P128, NT, 6])
        both = sb("a_both", [P128, NT])
        gap = sb("a_gap", [P128, NT])
        gap2 = sb("a_gap2", [P128, NT])
        square = sb("a_square", [P128, NT])
        mse = sb("a_mse", [P128, NT])
        mean = sb("a_mean", [P128, NT])
        ve = sb("a_ve", [P128, NT])
        sd = sb("a_sd", [P128, NT])
        r0 = sb("a_r0", [P128, NT])
        r1 = sb("a_r1", [P128, NT])
        r2 = sb("a_r2", [P128, NT])
        r3 = sb("a_r3", [P128, NT])
        rstd = sb("a_rstd", [P128, NT])
        xThl = sb("a_xThl", [P128, 2, KT, T], F32R)
        lg = sb("a_lg", [E, T])
        pT = ps("a_pT", [P128, KT, T])
        pL = ps("a_pL", [P128, T])
        pG = ps("a_pG", [P128, BANK])

        w_loaded = sem("a_w_loaded")
        wo_loaded = sem("a_wo_loaded")
        g_loaded = sem("a_g_loaded")
        x_loaded = sem("a_x_loaded")
        ident_made = sem("a_ident_made")
        w_hi = sem("a_w_hi")
        w_lo = sem("a_w_lo")
        wo_hi = sem("a_wo_hi")
        wo_lo = sem("a_wo_lo")
        g_trans = sem("a_g_trans")
        g_zero = sem("a_g_zero")
        g_copied = sem("a_g_copied")
        g_hi = sem("a_g_hi")
        g_lo = sem("a_g_lo")
        stat_done = sem("a_stat_done")
        sqrt_done = sem("a_sqrt_done")
        xn_done = sem("a_xn_done")
        xt_done = sem("a_xt_done")
        xt_hi = sem("a_xt_hi")
        xt_lo = sem("a_xt_lo")
        logit_done = sem("a_logit_done")
        lg_done = sem("a_lg_done")
        w_stored = sem("a_w_stored")
        b_stored = sem("a_b_stored")
        STAT = 9
        STORES = 4

        block = ctx.enter_context(nc.Block())

        @block.sync
        def _(sp):
            sp.dma_start(gw[:, :], gate_w).then_inc(g_loaded, 16)
            sp.dma_start(gb[:, :], gate_b.rearrange("(e a) -> e a", a=1)).then_inc(g_loaded, 16)
            with sp.Fori(0, B) as b:
                sp.wait_ge(xn_done, b * NT)
                sp.dma_start(xin[:, :, :], x[b, :, :].rearrange("(t p) c -> p t c", p=P128)).then_inc(x_loaded, 16)
                sp.wait_ge(xn_done, (b + 1) * NT)
                sp.dma_start(xn_s[b, :, :, :], xn[:, :, :]).then_inc(b_stored, 16)
                sp.wait_ge(xt_hi, b + 1)
                sp.dma_start(xt_s[b, :, 0, :, :], xThl[:, 0, :, :].bitcast(F32)).then_inc(b_stored, 16)
                sp.wait_ge(xt_lo, b + 1)
                sp.dma_start(xt_s[b, :, 1, :, :], xThl[:, 1, :, :].bitcast(F32)).then_inc(b_stored, 16)
                sp.wait_ge(lg_done, b + 1)
                sp.dma_start(logit_s[b, :, :], lg[:, :]).then_inc(b_stored, 16)
            sp.wait_ge(b_stored, B * STORES * 16)
            sp.wait_ge(w_stored, 48)

        @block.scalar
        def _(act):
            for n, w in enumerate((wq, wk, wv)):
                act.dma_start(wraw[:, n, :, :], w.rearrange("(k p) n -> p k n", p=P128)).then_inc(w_loaded, 16)
            act.dma_start(woraw[:, :, :], wo.rearrange("(k p) n -> p k n", p=P128)).then_inc(wo_loaded, 16)
            with act.Fori(0, B) as b:
                act.wait_ge(stat_done, b * STAT + 4)
                act.activation(sd[:, :], ve[:, :], ACT.Sqrt).then_inc(sqrt_done, 1)
                for k in range(KT):
                    act.wait_ge(xt_done, b * KT + k + 1)
                    hi = act.activation(xThl[:, 0, k, :], pT[:, k, :], ACT.Copy)
                hi.then_inc(xt_hi, 1)
                act.wait_ge(logit_done, b + 1)
                act.activation(lg[:, :], pL[0:E, :], ACT.Identity, bias=gb[:, :]).then_inc(lg_done, 1)
            act.wait_ge(w_lo, 3)
            act.dma_start(w_s.rearrange("r p h k n -> p r (h k n)"),
                          whl[:, :, :, :, :].rearrange("p r h k n -> p r (h k n)").bitcast(F32)).then_inc(w_stored, 16)
            act.wait_ge(wo_lo, 1)
            act.dma_start(wo_s[:, 0, :, :], wohl[:, 0, :, :].bitcast(F32)).then_inc(w_stored, 16)
            act.dma_start(wo_s[:, 1, :, :], wohl[:, 1, :, :].bitcast(F32)).then_inc(w_stored, 16)
            act.wait_ge(w_stored, 48)

        @block.gpsimd
        def _(pool):
            build_identity(pool, ident[:, :], ident_made, 0)
            pool.memset(gT[:, :, :], 0.0).then_inc(g_zero, 1)
            pool.wait_ge(w_loaded, 48)
            for n in range(3):
                for k in range(KT):
                    last = pool.tensor_scalar(whl[:, :, 0, k, n * P128:(n + 1) * P128],
                                              wraw[:, n, k, :].rearrange("p (r c) -> p r c", c=P128),
                                              SCALE if n == 0 else 1.0, 1.0, ALU.mult, ALU.mult)
                last.then_inc(w_hi, 1)
            pool.wait_ge(wo_loaded, 16)
            pool.tensor_copy(wohl[:, 0, :, :], woraw[:, :, :]).then_inc(wo_hi, 1)

        @block.vector
        def _(dve):
            dve.wait_ge(g_trans, 1)
            dve.wait_ge(g_zero, 1)
            dve.tensor_copy(gT[:, :, 0:E], pG[:, 0:KT * E].rearrange("p (k e) -> p k e", k=KT)).then_inc(g_copied, 1)
            dve.wait_ge(g_copied, 1)
            dve.tensor_copy(gThl[:, 0, :, :], gT[:, :, :]).then_inc(g_hi, 1)
            dve.wait_ge(g_hi, 1)
            dve.tensor_tensor(gThl[:, 1, :, :], gT[:, :, :], gThl[:, 0, :, :].bitcast(F32), ALU.subtract).then_inc(g_lo, 1)
            with dve.Fori(0, B) as b:
                dve.wait_ge(x_loaded, (b + 1) * 16)
                for t in range(NT):
                    st = dve.bn_stats(stats[:, t, :], xin[:, t, :])
                st.then_inc(stat_done, 1)
                dve.wait_ge(stat_done, b * STAT + 1)
                dve.tensor_tensor(both[:, :], stats[:, :, 1], stats[:, :, 4], ALU.add)
                dve.tensor_tensor(gap[:, :], stats[:, :, 1], stats[:, :, 4], ALU.subtract)
                dve.tensor_tensor(square[:, :], stats[:, :, 2], stats[:, :, 5], ALU.add).then_inc(stat_done, 1)
                dve.wait_ge(stat_done, b * STAT + 2)
                dve.tensor_scalar(mean[:, :], both[:, :], 0.5, None, ALU.mult)
                dve.tensor_tensor(gap2[:, :], gap[:, :], gap[:, :], ALU.mult)
                dve.tensor_scalar(mse[:, :], square[:, :], 1.0 / C, EPS, ALU.mult, ALU.add).then_inc(stat_done, 1)
                dve.wait_ge(stat_done, b * STAT + 3)
                dve.scalar_tensor_tensor(ve[:, :], gap2[:, :], 0.25, mse[:, :], ALU.mult, ALU.add).then_inc(stat_done, 1)
                dve.wait_ge(sqrt_done, b + 1)
                dve.reciprocal(r0[:, :], sd[:, :]).then_inc(stat_done, 1)
                dve.wait_ge(stat_done, b * STAT + 5)
                dve.tensor_tensor(r1[:, :], r0[:, :], r0[:, :], ALU.mult).then_inc(stat_done, 1)
                dve.wait_ge(stat_done, b * STAT + 6)
                dve.tensor_tensor(r2[:, :], r1[:, :], ve[:, :], ALU.mult).then_inc(stat_done, 1)
                dve.wait_ge(stat_done, b * STAT + 7)
                dve.tensor_scalar(r3[:, :], r2[:, :], -0.5, 1.5, ALU.mult, ALU.add).then_inc(stat_done, 1)
                dve.wait_ge(stat_done, b * STAT + 8)
                dve.tensor_tensor(rstd[:, :], r3[:, :], r0[:, :], ALU.mult).then_inc(stat_done, 1)
                dve.wait_ge(stat_done, b * STAT + 9)
                dve.wait_ge(b_stored, b * STORES * 16)
                for t in range(NT):
                    dve.tensor_scalar(xn[:, t, :], xin[:, t, :], mean[:, t:t + 1], rstd[:, t:t + 1],
                                      ALU.subtract, ALU.mult).then_inc(xn_done, 1)
                for k in range(KT):
                    dve.wait_ge(xt_done, b * KT + k + 1)
                    dve.wait_ge(xt_hi, b + 1)
                    lo = dve.tensor_tensor(xThl[:, 1, k, :], pT[:, k, :], xThl[:, 0, k, :].bitcast(F32), ALU.subtract)
                lo.then_inc(xt_lo, 1)
            for n in range(3):
                dve.wait_ge(w_hi, n + 1)
                for k in range(KT):
                    last = dve.scalar_tensor_tensor(
                        whl[:, :, 1, k, n * P128:(n + 1) * P128], wraw[:, n, k, :].rearrange("p (r c) -> p r c", c=P128),
                        SCALE if n == 0 else 1.0, whl[:, :, 0, k, n * P128:(n + 1) * P128].bitcast(F32),
                        ALU.mult, ALU.subtract)
                last.then_inc(w_lo, 1)
            dve.wait_ge(wo_hi, 1)
            dve.tensor_tensor(wohl[:, 1, :, :], woraw[:, :, :], wohl[:, 0, :, :].bitcast(F32), ALU.subtract).then_inc(wo_lo, 1)

        @block.tensor
        def _(pe):
            pe.wait_ge(ident_made, 2)
            pe.wait_ge(g_loaded, 32)
            for k in range(KT):
                tr = pe.transpose(pG[:, k * E:(k + 1) * E], gw[:, k * P128:(k + 1) * P128], ident[0:E, 0:E])
            tr.then_inc(g_trans, 1)
            pe.wait_ge(g_lo, 1)
            with pe.Fori(0, B) as b:
                pe.wait_ge(xt_lo, b)
                for k in range(KT):
                    for t in range(NT):
                        pe.wait_ge(xn_done, b * NT + t + 1)
                        tr = pe.transpose(pT[:, k, t * P128:(t + 1) * P128], xn[:, t, k * P128:(k + 1) * P128], ident[:, :])
                    tr.then_inc(xt_done, 1)
                pe.wait_ge(xt_lo, b + 1)
                pe.wait_ge(lg_done, b)
                for c in range(T // BANK):
                    n = 0
                    for k in range(KT):
                        for hg, hx in ((0, 0), (0, 1), (1, 0)):
                            mm = pe.matmul(pL[:, c * BANK:(c + 1) * BANK], gThl[:, hg, k, :],
                                           xThl[:, hx, k, c * BANK:(c + 1) * BANK], start=(n == 0), stop=(n == 3 * KT - 1))
                            n += 1
                mm.then_inc(logit_done, 1)


def route_block(nc, logit_s, xn_s, wsp_s, mgt_s):
    with ExitStack() as ctx:
        def sb(name, shape, dt=F32):
            return ctx.enter_context(nc.sbuf_tensor(name, shape, dt))

        def ps(name, shape):
            return ctx.enter_context(nc.psum_tensor(name, shape, F32))

        def sem(name):
            return ctx.enter_context(nc.semaphore(name))

        ident = sb("r_ident", [P128, P128])
        L = sb("r_L", [P128, T])
        Lr = sb("r_Lr", [P128, T])
        Ex = sb("r_Ex", [P128, T])
        taken = sb("r_taken", [P128, T])
        W = sb("r_W", [P128, T])
        WT = sb("r_WT", [P128, NT, P128])
        xn = sb("r_xn", [P128, B, NT, C])
        top = sb("r_top", [P128, 8])
        nmax = sb("r_nmax", [P128, 1])
        total = sb("r_total", [P128, 1])
        rtotal = sb("r_rtotal", [P128, 1])
        mg = sb("r_mg", [P128, C])
        mgT = sb("r_mgT", [P128, KT, P128])
        pW = ps("r_pW", [P128, T])
        pM = ps("r_pM", [P128, BANK])
        pMT = ps("r_pMT", [P128, BANK])

        l_loaded = sem("r_l_loaded")
        xn_loaded = sem("r_xn_loaded")
        ident_made = sem("r_ident_made")
        dv = sem("r_dv")
        ex_done = sem("r_ex_done")
        wt_done = sem("r_wt_done")
        wt_copied = sem("r_wt_copied")
        mg_done = sem("r_mg_done")
        mgt_done = sem("r_mgt_done")
        stored = sem("r_stored")
        block = ctx.enter_context(nc.Block())

        @block.sync
        def _(sp):
            sp.dma_start(L[:, :], logit_s.rearrange("b e t -> (b e) t")).then_inc(l_loaded, 16)
            sp.dma_start(xn[:, :, :, :].rearrange("p b t c -> p b (t c)"),
                         xn_s.rearrange("b p t c -> p b (t c)")).then_inc(xn_loaded, 16)
            sp.wait_ge(dv, 6)
            sp.dma_start(wsp_s.rearrange("b e t -> (b e) t"), W[:, :]).then_inc(stored, 16)
            sp.wait_ge(dv, 8)
            sp.dma_start(mgt_s, mgT[:, :, :]).then_inc(stored, 16)
            sp.wait_ge(stored, 32)

        @block.gpsimd
        def _(pool):
            build_identity(pool, ident[:, :], ident_made, 0)

        @block.scalar
        def _(act):
            act.wait_ge(dv, 2)
            act.activation(Ex[:, :], L[:, :], ACT.Exp, bias=nmax[:, :], accum_out=total[:, :]).then_inc(ex_done, 1)
            act.wait_ge(wt_done, 1)
            act.activation(WT[:, :, :].rearrange("p t m -> p (t m)"), pW[:, :], ACT.Copy).then_inc(wt_copied, 1)

        @block.vector
        def _(dve):
            dve.wait_ge(l_loaded, 16)
            dve.max(top[:, :], L[:, :]).then_inc(dv, 1)
            dve.wait_ge(dv, 1)
            dve.tensor_scalar(nmax[:, :], top[:, 0:1], -1.0, None, ALU.mult).then_inc(dv, 1)
            dve.match_replace(out=Lr[:, :], in_to_replace=top[:, :], in_values=L[:, :], imm_value=USED).then_inc(dv, 1)
            dve.wait_ge(dv, 3)
            dve.tensor_tensor(taken[:, :], Lr[:, :], L[:, :], ALU.not_equal).then_inc(dv, 1)
            dve.wait_ge(ex_done, 1)
            dve.reciprocal(rtotal[:, :], total[:, :]).then_inc(dv, 1)
            dve.wait_ge(dv, 5)
            dve.scalar_tensor_tensor(W[:, :], Ex[:, :], rtotal[:, :], taken[:, :], ALU.mult, ALU.mult).then_inc(dv, 1)
            dve.wait_ge(mg_done, 1)
            dve.tensor_copy(mg[:, :], pM[:, 0:C]).then_inc(dv, 1)
            dve.wait_ge(mgt_done, 1)
            dve.tensor_copy(mgT[:, :, :].rearrange("p k m -> p (k m)"), pMT[:, 0:KT * P128]).then_inc(dv, 1)

        @block.tensor
        def _(pe):
            pe.wait_ge(ident_made, 2)
            pe.wait_ge(dv, 6)
            for t in range(NT):
                tr = pe.transpose(pW[:, t * P128:(t + 1) * P128], W[:, t * P128:(t + 1) * P128], ident[:, :])
            tr.then_inc(wt_done, 1)
            pe.wait_ge(wt_copied, 1)
            pe.wait_ge(xn_loaded, 16)
            for t in range(NT):
                for b in range(B):
                    mm = pe.matmul(pM[b * E:(b + 1) * E, 0:C], WT[:, t, b * E:(b + 1) * E], xn[:, b, t, :],
                                   start=(t == 0), stop=(t == NT - 1))
            mm.then_inc(mg_done, 1)
            pe.wait_ge(dv, 7)
            for k in range(KT):
                tr = pe.transpose(pMT[:, k * P128:(k + 1) * P128], mg[:, k * P128:(k + 1) * P128], ident[:, :])
            tr.then_inc(mgt_done, 1)


def experts_block(nc, w1, w2, mgt_s, o_s):
    with ExitStack() as ctx:
        def sb(name, shape, dt=F32):
            return ctx.enter_context(nc.sbuf_tensor(name, shape, dt))

        def ps(name, shape):
            return ctx.enter_context(nc.psum_tensor(name, shape, F32))

        def sem(name):
            return ctx.enter_context(nc.semaphore(name))

        ident = sb("e_ident", [P128, P128])
        fold = sb("e_fold", [P128, 32])
        mgT = sb("e_mgT", [P128, KT, B, E])
        mT = sb("e_mT", [P128, 2, KT, 32])
        w1t = sb("e_w1t", [P128, 2, KT, HID])
        w2t = sb("e_w2t", [P128, 2, 4, 2, C])
        b1 = sb("e_b1", [P128, 2, Q4])
        b2 = sb("e_b2", [B, 2, C])
        hb = sb("e_hb", [P128, 2, Q4])
        g = sb("e_g", [P128, 2, Q4])
        hT = sb("e_hT", [P128, 2, 2, P128])
        part = sb("e_part", [P128, 2, C])
        oe = sb("e_oe", [B, 2, C])
        pH = [ps(f"e_pH{i}", [P128, BANK]) for i in range(2)]
        pHT = [ps(f"e_pHT{i}", [P128, BANK]) for i in range(2)]
        pO = [ps(f"e_pO{i}", [P128, BANK]) for i in range(2)]
        pF = [ps(f"e_pF{i}", [P128, BANK]) for i in range(2)]

        m_loaded = sem("e_m_loaded")
        ident_made = sem("e_ident_made")
        fold_made = sem("e_fold_made")
        zeroed = sem("e_zeroed")
        w1_loaded = [sem(f"e_w1_loaded{i}") for i in range(2)]
        w2_loaded = [sem(f"e_w2_loaded{i}") for i in range(2)]
        b_loaded = [sem(f"e_b_loaded{i}") for i in range(2)]
        mT_done = sem("e_mT_done")
        h_done = sem("e_h_done")
        hb_done = sem("e_hb_done")
        g_done = sem("e_g_done")
        hT_done = sem("e_hT_done")
        hT_copied = sem("e_hT_copied")
        part_done = sem("e_part_done")
        part_copied = sem("e_part_copied")
        fold_done = sem("e_fold_done")
        oe_done = sem("e_oe_done")
        oe_stored = [sem(f"e_oe_stored{i}") for i in range(2)]
        block = ctx.enter_context(nc.Block())

        def load_w1(q, e, par):
            q.dma_start(w1t[:, par, :, :], w1[e, 0:C, :].rearrange("(k p) n -> p k n", p=P128)).then_inc(w1_loaded[par], 16)

        def load_w2(q, e, par):
            q.dma_start(w2t[:, par, :, :, :].rearrange("p j c n -> p j (c n)"),
                        w2[e, 0:HID, :].rearrange("(j p c) n -> p j (c n)", p=P128, c=2)).then_inc(w2_loaded[par], 16)

        def load_bias(q, e, par):
            for j in range(4):
                q.dma_start(b1[32 * j:32 * j + B, par, :],
                            w1[e, C:C + 1, j * Q4:(j + 1) * Q4].to_broadcast([B, Q4])).then_inc(b_loaded[par], 16)
            q.dma_start(b2[:, par, :], w2[e, HID:HID + 1, :].to_broadcast([B, C])).then_inc(b_loaded[par], 16)

        BIAS = 5 * 16

        @block.sync
        def _(sp):
            sp.dma_start(mgT[:, :, :, :].rearrange("p k b e -> p (k b e)"),
                         mgt_s.rearrange("p k m -> p (k m)")).then_inc(m_loaded, 16)
            for par in range(2):
                load_w1(sp, par, par)
                load_w2(sp, par, par)
            with sp.Fori(0, E // 2 - 1) as it:
                for par in range(2):
                    e = it * 2 + par
                    sp.wait_ge(h_done, e + 1)
                    load_w1(sp, e + 2, par)
                    sp.wait_ge(part_done, e + 1)
                    load_w2(sp, e + 2, par)

        @block.scalar
        def _(act):
            act.wait_ge(zeroed, 3)
            for par in range(2):
                load_bias(act, par, par)

            def steps(e, par, more):
                act.wait_ge(hb_done, e + 1)
                act.activation(g[:, par, :], hb[:, par, :], ACT.Gelu).then_inc(g_done, 1)
                act.wait_ge(part_done, e + 1)
                act.activation(part[:, par, :], pO[par][:, 0:C], ACT.Copy).then_inc(part_copied, 1)
                act.wait_ge(oe_done, e + 1)
                act.dma_start(o_s[:, e, :], oe[:, par, :]).then_inc(oe_stored[par], 16)
                if more:
                    load_bias(act, e + 2, par)

            with act.Fori(0, E // 2 - 1) as it:
                for par in range(2):
                    steps(it * 2 + par, par, True)
            for par in range(2):
                steps(E - 2 + par, par, False)
            for par in range(2):
                act.wait_ge(oe_stored[par], E // 2 * 16)

        @block.gpsimd
        def _(pool):
            pool.memset(b1[:, :, :], 0.0).then_inc(zeroed, 1)
            pool.memset(mT[:, :, :, :], 0.0).then_inc(zeroed, 1)
            pool.memset(hb[:, :, :], 0.0).then_inc(zeroed, 1)
            build_identity(pool, ident[:, :], ident_made, 0)
            pool.memset(fold[:, :], 0.0).then_inc(fold_made, 1)
            for j in range(4):
                pool.wait_ge(fold_made, j + 1)
                pool.affine_select(out=fold[:, 0:B], in_=fold[:, 0:B], compare_op=ALU.not_equal, fill=1.0,
                                   base=-32 * j, pattern=[[-1, B]], channel_multiplier=1).then_inc(fold_made, 1)

        @block.vector
        def _(dve):
            dve.wait_ge(m_loaded, 16)
            dve.wait_ge(zeroed, 3)

            def first(e, par, reuse):
                if reuse:
                    dve.wait_ge(h_done, e - 1)
                dve.tensor_copy(mT[:, par, :, 0:B], mgT[:, :, :, e]).then_inc(mT_done, 1)

            def rest(e, par, it):
                dve.wait_ge(h_done, e + 1)
                dve.wait_ge(b_loaded[par], (it + 1) * BIAS)
                dve.tensor_tensor(hb[:, par, :], pH[par][:, 0:Q4], b1[:, par, :], ALU.add).then_inc(hb_done, 1)
                dve.wait_ge(hT_done, e + 1)
                dve.tensor_copy(hT[:, par, :, :].rearrange("p c m -> p (c m)"), pHT[par][:, 0:2 * P128]).then_inc(hT_copied, 1)
                dve.wait_ge(fold_done, e + 1)
                dve.tensor_tensor(oe[:, par, :], pF[par][0:B, 0:C], b2[:, par, :], ALU.add).then_inc(oe_done, 1)

            first(0, 0, False)
            first(1, 1, False)
            rest(0, 0, 0)
            first(2, 0, True)
            rest(1, 1, 0)
            with dve.Fori(1, E // 2 - 1) as it:
                first(it * 2 + 1, 1, True)
                dve.wait_ge(oe_stored[0], it * 16)
                rest(it * 2, 0, it)
                first(it * 2 + 2, 0, True)
                dve.wait_ge(oe_stored[1], it * 16)
                rest(it * 2 + 1, 1, it)
            first(E - 1, 1, True)
            dve.wait_ge(oe_stored[0], (E // 2 - 1) * 16)
            rest(E - 2, 0, E // 2 - 1)
            dve.wait_ge(oe_stored[1], (E // 2 - 1) * 16)
            rest(E - 1, 1, E // 2 - 1)

        @block.tensor
        def _(pe):
            pe.wait_ge(ident_made, 2)
            pe.wait_ge(fold_made, 5)

            def layer1(e, par, it, reuse):
                pe.wait_ge(mT_done, e + 1)
                pe.wait_ge(w1_loaded[par], (it + 1) * 16)
                if reuse:
                    pe.wait_ge(hb_done, e - 1)
                for k in range(KT):
                    for j in range(4):
                        mm = pe.matmul(pH[par][32 * j:32 * j + 32, 0:Q4], mT[:, par, k, :],
                                       w1t[:, par, k, j * Q4:(j + 1) * Q4], start=(k == 0), stop=(k == KT - 1))
                mm.then_inc(h_done, 1)

            def layer2(e, par, it, reuse):
                pe.wait_ge(g_done, e + 1)
                if reuse:
                    pe.wait_ge(hT_copied, e - 1)
                for c in range(2):
                    tr = pe.transpose(pHT[par][:, c * P128:(c + 1) * P128], g[:, par, c::2], ident[:, :])
                tr.then_inc(hT_done, 1)
                pe.wait_ge(hT_copied, e + 1)
                pe.wait_ge(w2_loaded[par], (it + 1) * 16)
                if reuse:
                    pe.wait_ge(part_copied, e - 1)
                for c in range(2):
                    for j in range(4):
                        mm = pe.matmul(pO[par][32 * j:32 * j + 32, 0:C], hT[:, par, c, 32 * j:32 * j + 32],
                                       w2t[:, par, j, c, :], start=(c == 0), stop=(c == 1))
                mm.then_inc(part_done, 1)
                pe.wait_ge(part_copied, e + 1)
                if reuse:
                    pe.wait_ge(oe_done, e - 1)
                pe.matmul(pF[par][0:32, 0:C], fold[:, :], part[:, par, :], start=True, stop=True).then_inc(fold_done, 1)

            layer1(0, 0, 0, False)
            layer1(1, 1, 0, False)
            layer2(0, 0, 0, False)
            layer1(2, 0, 1, True)
            layer2(1, 1, 0, False)
            with pe.Fori(1, E // 2 - 1) as it:
                layer1(it * 2 + 1, 1, it, True)
                layer2(it * 2, 0, it, True)
                layer1(it * 2 + 2, 0, it + 1, True)
                layer2(it * 2 + 1, 1, it, True)
            layer1(E - 1, 1, E // 2 - 1, True)
            layer2(E - 2, 0, E // 2 - 1, True)
            layer2(E - 1, 1, E // 2 - 1, True)


def attend_block(nc, x, bo, rot_cos, rot_sin, xt_s, w_s, wo_s, wsp_s, o_s, out):
    CH = [(i + 4) // 4 for i in range(NT)]
    CHUNKS = 2 * sum(CH)
    STEPS = 2 * NT

    def chunk0(i, h):
        return 2 * sum(CH[:i]) + h * CH[i]

    with ExitStack() as ctx:
        def sb(name, shape, dt=F32):
            return ctx.enter_context(nc.sbuf_tensor(name, shape, dt))

        def ps(name, shape):
            return ctx.enter_context(nc.psum_tensor(name, shape, F32))

        def sem(name):
            return ctx.enter_context(nc.semaphore(name))

        ident = sb("t_ident", [P128, P128])
        identr = sb("t_identr", [P128, P128], F32R)
        identb = sb("t_identb", [P128, P128], BF16)
        maskb = sb("t_maskb", [P128, P128], BF16)
        cos = sb("t_cos", [P128, NT, DH])
        sin = sb("t_sin", [P128, NT, DH])
        bob = sb("t_bob", [P128, C])
        xT = sb("t_xT", [P128, NT, 2, KT, P128], F32R)
        w = sb("t_w", [P128, 2, 2, KT, QKV], F32R)
        wo = sb("t_wo", [P128, 2, PAIRS, C], F32R)
        QH = sb("t_QH", [P128, 2, 2, T], F32R)
        QL = sb("t_QL", [P128, 2, 2, T], F32R)
        KS = sb("t_KS", [P128, 2, 2, T], F32R)
        V = sb("t_V", [P128, 2, NT, P128])
        rc = sb("t_rc", [P128, 2, 2 * P128])
        rs = sb("t_rs", [P128, 2, 2 * P128])
        rq = sb("t_rq", [P128, 2, 2, 2, DH])
        rk = sb("t_rk", [P128, 2, 2, DH])
        kk = sb("t_kk", [P128, 2, 2, 2, DH], F32R)
        nmax = sb("t_nmax", [P128, 2])
        psum_row = sb("t_sum", [P128, 2, 2])
        recip = sb("t_recip", [P128, 2, 2])
        rep = sb("t_rep", [P128, 2, 2, DH])
        Pr = sb("t_Pr", [P128, 2, T])
        PT = sb("t_PT", [P128, 2, 2, T])
        rT = sb("t_rT", [P128, P128])
        OT = sb("t_OT", [P128, PAIRS, T])
        oh = sb("t_oh", [P128, 2, PAIRS, P128], F32R)
        ol = sb("t_ol", [P128, 2, PAIRS, P128], F32R)
        wsp = sb("t_wsp", [E, T])
        oe = sb("t_oe", [E, C])
        xin = sb("t_xin", [P128, 2, C])
        xb = sb("t_xb", [P128, 2, C])
        yt = sb("t_yt", [P128, 2, C])
        pS = [ps(f"t_pS{i}", [P128, T]) for i in range(2)]
        pT = [ps(f"t_pT{i}", [P128, BANK]) for i in range(2)]
        pO = ps("t_pO", [P128, BANK])
        pP = ps("t_pP", [P128, BANK])

        table_loaded = sem("t_table_loaded")
        wo_loaded = sem("t_wo_loaded")
        bo_loaded = sem("t_bo_loaded")
        const_made = sem("t_const_made")
        identr_made = sem("t_identr_made")
        xt_loaded = [sem(f"t_xt_loaded{t}") for t in range(NT)]
        w_loaded = [sem(f"t_w_loaded{i}") for i in range(2)]
        recip_done = sem("t_recip_done")
        moe_loaded = sem("t_moe_loaded")
        x_loaded = [sem(f"t_x_loaded{i}") for i in range(2)]
        proj_done = sem("t_proj_done")
        rope_done = sem("t_rope_done")
        rk_done = sem("t_rk_done")
        kh_done = sem("t_kh_done")
        rot_done = sem("t_rot_done")
        stackT_done = sem("t_stackT_done")
        stack_hi = sem("t_stack_hi")
        stack_lo = sem("t_stack_lo")
        s_done = sem("t_s_done")
        max_done = sem("t_max_done")
        exp_done = sem("t_exp_done")
        t_done = sem("t_t_done")
        evac_done = sem("t_evac_done")
        rep_done = sem("t_rep_done")
        pv_done = sem("t_pv_done")
        rt_copied = sem("t_rt_copied")
        o_done = sem("t_o_done")
        oh_done = sem("t_oh_done")
        ol_done = sem("t_ol_done")
        xb_done = sem("t_xb_done")
        y_mm = sem("t_y_mm")
        y_done = sem("t_y_done")
        y_stored = [sem(f"t_y_stored{i}") for i in range(2)]
        block = ctx.enter_context(nc.Block())

        LAST = B * PAIRS - 1

        def first_bank(t):
            return pS[t // 2 % 2][:, t % 2 * BANK:(t % 2 + 1) * BANK]

        def pairs(engine, attend):
            attend(0, 0, 0, True, False, None, None)
            with engine.Fori(0, B - 1) as b:
                with engine.Fori(0, PAIRS // 2 - 1) as g:
                    attend(b * PAIRS + g * 2 + 1, g * 2 + 1, 1, False, False, None, None)
                    attend(b * PAIRS + g * 2 + 2, g * 2 + 2, 0, False, False, None, None)
                attend(b * PAIRS + PAIRS - 1, PAIRS - 1, 1, False, False, None, b)
                attend(b * PAIRS + PAIRS, 0, 0, False, False, b, None)
            with engine.Fori(0, PAIRS // 2 - 1) as g:
                attend((B - 1) * PAIRS + g * 2 + 1, g * 2 + 1, 1, False, False, None, None)
                attend((B - 1) * PAIRS + g * 2 + 2, g * 2 + 2, 0, False, False, None, None)
            attend(LAST, PAIRS - 1, 1, False, True, None, None)

        @block.sync
        def _(sp):
            sp.dma_start(cos[:, :, :], rot_cos.rearrange("(t p) d -> p t d", p=P128)).then_inc(table_loaded, 16)
            sp.dma_start(sin[:, :, :], rot_sin.rearrange("(t p) d -> p t d", p=P128)).then_inc(table_loaded, 16)

            def load_xt(b, t):
                sp.dma_start(xT[:, t, :, :, :].bitcast(F32), xt_s[b, :, :, :, t * P128:(t + 1) * P128]).then_inc(xt_loaded[t], 16)

            def load_w(p, par):
                sp.dma_start(w[:, par, :, :, :].bitcast(F32), w_s[p, :, :, :, :]).then_inc(w_loaded[par], 16)

            load_w(0, 0)
            for t in range(NT):
                load_xt(0, t)
            load_w(1, 1)

            def reload(P, p, par):
                sp.wait_ge(proj_done, (P + 1) * NT)
                load_w(p, par)

            with sp.Fori(0, B - 1) as b:
                with sp.Fori(0, PAIRS // 2 - 1) as g:
                    for par in range(2):
                        reload(b * PAIRS + g * 2 + par, g * 2 + 2 + par, par)
                reload(b * PAIRS + PAIRS - 2, 0, 0)
                for t in range(NT):
                    sp.wait_ge(proj_done, (b * PAIRS + PAIRS - 1) * NT + t + 1)
                    load_xt(b + 1, t)
                reload(b * PAIRS + PAIRS - 1, 1, 1)
            with sp.Fori(0, PAIRS // 2 - 1) as g:
                for par in range(2):
                    reload((B - 1) * PAIRS + g * 2 + par, g * 2 + 2 + par, par)

        @block.gpsimd
        def _(pool):
            build_identity(pool, ident[:, :], const_made, 0)
            pool.memset(maskb[:, :], 0.0).then_inc(const_made, 1)
            pool.wait_ge(const_made, 3)
            pool.affine_select(out=maskb[:, :], in_=maskb[:, :], compare_op=ALU.is_ge, fill=MASKED, base=0,
                               pattern=[[-1, P128]], channel_multiplier=1).then_inc(const_made, 1)
            pool.tensor_copy(identr[:, :], ident[:, :]).then_inc(identr_made, 1)
            pool.tensor_copy(identb[:, :], ident[:, :]).then_inc(identr_made, 1)

            def rotate(TI, u):
                pool.wait_ge(rope_done, TI + 1)
                cq = rc[:, u, 0:P128].rearrange("p (h d) -> p h d", h=2)
                sq = rs[:, u, 0:P128].rearrange("p (h d) -> p h d", h=2)
                ck = rc[:, u, P128:].rearrange("p (h d) -> p h d", h=2)
                sk = rs[:, u, P128:].rearrange("p (h d) -> p h d", h=2)
                pool.tensor_tensor(rk[:, u, :, :], ck, sk, ALU.add).then_inc(rk_done, 1)
                pool.tensor_tensor(rq[:, u, :, 0, :], cq, sq, ALU.add)
                pool.wait_ge(rk_done, TI + 1)
                pool.tensor_tensor(rq[:, u, :, 1, :], cq, sq, ALU.add)
                pool.tensor_copy(kk[:, u, :, 0, :], rk[:, u, :, :]).then_inc(kh_done, 1)
                pool.wait_ge(kh_done, TI + 1)
                pool.tensor_tensor(kk[:, u, :, 1, :], rk[:, u, :, :], kk[:, u, :, 0, :].bitcast(F32), ALU.subtract).then_inc(rot_done, 1)

            def prologue():
                for t in range(NT):
                    if t >= 2:
                        pool.wait_ge(stackT_done, t - 1)
                    rotate(t, t % 2)

            def input_and_bias(y, t):
                u = t % 2
                pool.wait_ge(x_loaded[u], (y * (NT // 2) + t // 2 + 1) * 16)
                if t >= 2:
                    pool.wait_ge(y_done, y * NT + t - 1)
                pool.tensor_tensor(xb[:, u, :], xin[:, u, :], bob[:, :], ALU.add).then_inc(xb_done, 1)

            def attend(P, p, par, first, last, yb, crossing):
                for t in range(NT):
                    if yb is not None:
                        input_and_bias(yb, t)
                    if not last:
                        TI = (P + 1) * NT + t
                        pool.wait_ge(stackT_done, TI - 1)
                        rotate(TI, t % 2)

            def tail():
                for t in range(NT):
                    input_and_bias(B - 1, t)

            pool.dma_start(bob[:, :], bo.rearrange("(a n) -> a n", a=1).to_broadcast([P128, C])).then_inc(bo_loaded, 16)
            pool.wait_ge(bo_loaded, 16)
            prologue()
            pairs(pool, attend)
            tail()

        @block.scalar
        def _(act):
            act.dma_start(wo[:, :, :, :].bitcast(F32), wo_s).then_inc(wo_loaded, 16)

            def exp(SI, i, h):
                s = (2 * i + h) % 2
                act.wait_ge(max_done, SI + 1)
                act.activation(Pr[:, s, 0:(i + 1) * P128], pS[s][:, 0:(i + 1) * P128], ACT.Exp, bias=nmax[:, s:s + 1],
                               accum_out=psum_row[:, i % 2, h:h + 1]).then_inc(exp_done, 1)

            def evac(P, i, h):
                for c in range(CH[i]):
                    n = chunk0(i, h) + c
                    lo, hi = c * BANK, min((c + 1) * BANK, (i + 1) * P128)
                    act.wait_ge(t_done, P * CHUNKS + n + 1)
                    act.activation(PT[:, i % 2, h, lo:hi], pT[n % 2][:, 0:hi - lo], ACT.Copy).then_inc(evac_done, 1)

            def stack(TI, t, par):
                act.wait_ge(stackT_done, TI + 1)
                act.activation(KS[:, par, :, t * P128:(t + 1) * P128],
                               pP[:, 2 * P128:].rearrange("p (h n) -> p h n", h=2), ACT.Copy)
                act.activation(QH[:, par, :, t * P128:(t + 1) * P128],
                               pP[:, 0:2 * P128].rearrange("p (h n) -> p h n", h=2), ACT.Copy).then_inc(stack_hi, 1)

            def prologue():
                for t in range(NT - 1):
                    stack(t, t, 0)
                exp(0, 0, 0)

            def load_x(y, t):
                act.dma_start(xin[:, t % 2, :], x[y, t * P128:(t + 1) * P128, :]).then_inc(x_loaded[t % 2], 16)

            def start_output(y):
                act.dma_start(wsp[:, :], wsp_s[y, :, :]).then_inc(moe_loaded, 16)
                act.dma_start(oe[:, :], o_s[y, :, :]).then_inc(moe_loaded, 16)
                load_x(y, 0)
                load_x(y, 1)

            def rounded(y, t):
                if t == NT - 1:
                    act.wait_ge(o_done, (y + 1) * PAIRS * NT)
                if t >= 2:
                    act.wait_ge(y_mm, y * NT + t - 1)
                act.activation(oh[:, t % 2, :, :], OT[:, :, t * P128:(t + 1) * P128], ACT.Copy).then_inc(oh_done, 1)

            def store(y, t):
                u = t % 2
                act.wait_ge(y_done, y * NT + t + 1)
                act.dma_start(out[y, t * P128:(t + 1) * P128, :], yt[:, u, :]).then_inc(y_stored[u], 16)
                if t + 2 < NT:
                    act.wait_ge(xb_done, y * NT + t + 1)
                    load_x(y, t + 2)

            def attend(P, p, par, first, last, yb, crossing):
                if yb is not None:
                    start_output(yb)
                for i in range(NT):
                    exp(P * STEPS + 2 * i + 1, i, 1)
                    if not first or i >= 2:
                        act.wait_ge(pv_done, P * NT + i - 1)
                    evac(P, i, 0)
                    if yb is not None:
                        rounded(yb, i)
                    if i == 0:
                        stack(P * NT + NT - 1, NT - 1, par)
                    elif not last:
                        stack((P + 1) * NT + i - 1, i - 1, 1 - par)
                    if i + 1 < NT:
                        exp(P * STEPS + 2 * i + 2, i + 1, 0)
                    elif not last:
                        exp(P * STEPS + STEPS, 0, 0)
                    evac(P, i, 1)
                    if yb is not None and i > 0:
                        store(yb, i - 1)
                if yb is not None:
                    store(yb, NT - 1)

            def tail():
                act.wait_ge(o_done, B * PAIRS * NT)
                rounded(B - 1, 0)
                for t in range(NT):
                    if t + 1 < NT:
                        rounded(B - 1, t + 1)
                    store(B - 1, t)

            prologue()
            pairs(act, attend)
            start_output(B - 1)
            tail()
            for u in range(2):
                act.wait_ge(y_stored[u], B * NT // 2 * 16)

        @block.vector
        def _(dve):
            dve.wait_ge(table_loaded, 32)

            def rope(TI, t, par, bank):
                u = t % 2
                dve.wait_ge(proj_done, TI + 1)
                q2 = bank[:, 0:2 * P128]
                four = [P128, 4, DH]
                dve.tensor_tensor(rc[:, u, :].rearrange("p (g d) -> p g d", d=DH), q2.rearrange("p (g d) -> p g d", d=DH),
                                  cos[:, t, :].unsqueeze(1).to_broadcast(four), ALU.mult)
                for o in range(2):
                    dve.tensor_tensor(rs[:, u, :].rearrange("p (g d o) -> p g d o", d=DH // 2, o=2)[:, :, :, o],
                                      q2.rearrange("p (g d o) -> p g d o", d=DH // 2, o=2)[:, :, :, 1 - o],
                                      sin[:, t, o::2].unsqueeze(1).to_broadcast([P128, 4, DH // 2]), ALU.mult)
                dve.tensor_copy(V[:, par, t, :], bank[:, 2 * P128:QKV]).then_inc(rope_done, 1)

            def stack(TI, t, par):
                dve.wait_ge(stack_hi, TI + 1)
                dve.tensor_tensor(QL[:, par, :, t * P128:(t + 1) * P128], pP[:, 0:2 * P128].rearrange("p (h n) -> p h n", h=2),
                                  QH[:, par, :, t * P128:(t + 1) * P128].bitcast(F32), ALU.subtract).then_inc(stack_lo, 1)

            def row_max(SI, i, h):
                s = (2 * i + h) % 2
                dve.wait_ge(s_done, SI + 1)
                dve.tensor_reduce(nmax[:, s:s + 1], pS[s][:, 0:(i + 1) * P128], AX_X, ALU.max, negate=True).then_inc(max_done, 1)

            def reciprocals(OI, SI, i):
                dve.wait_ge(exp_done, SI + 1)
                dve.reciprocal(recip[:, i % 2, :], psum_row[:, i % 2, :]).then_inc(recip_done, 1)

            def replicate(OI, i):
                dve.wait_ge(recip_done, OI + 1)
                dve.tensor_scalar(rep[:, i % 2, :, :], recip[:, i % 2, :].unsqueeze(2).to_broadcast([P128, 2, DH]),
                                  1.0, None, ALU.mult).then_inc(rep_done, 1)

            def values(OI, p, i):
                dve.wait_ge(pv_done, OI + 1)
                dve.tensor_copy(rT[:, :], pO[:, P128:2 * P128]).then_inc(rt_copied, 1)
                dve.wait_ge(rt_copied, OI + 1)
                dve.tensor_tensor(OT[:, p, i * P128:(i + 1) * P128], pO[:, 0:P128], rT[:, :], ALU.mult).then_inc(o_done, 1)

            def prologue():
                for t in range(NT):
                    if t >= 2:
                        dve.wait_ge(rot_done, t - 1)
                    rope(t, t, 0, first_bank(t))
                    if t >= 1:
                        stack(t - 1, t - 1, 0)
                row_max(0, 0, 0)

            def rest(y, t):
                dve.wait_ge(oh_done, y * NT + t + 1)
                if t >= 2:
                    dve.wait_ge(y_mm, y * NT + t - 1)
                dve.tensor_tensor(ol[:, t % 2, :, :], OT[:, :, t * P128:(t + 1) * P128], oh[:, t % 2, :, :].bitcast(F32),
                                  ALU.subtract).then_inc(ol_done, 1)

            def output(y, t, bank):
                u = t % 2
                dve.wait_ge(y_mm, y * NT + t + 1)
                dve.wait_ge(xb_done, y * NT + t + 1)
                dve.wait_ge(y_stored[u], (y * (NT // 2) + t // 2) * 16)
                dve.tensor_tensor(yt[:, u, :], bank, xb[:, u, :], ALU.add).then_inc(y_done, 1)

            def attend(P, p, par, first, last, yb, crossing):
                for i in range(NT):
                    if i > 0:
                        reciprocals(P * NT + i - 1, P * STEPS + 2 * i - 1, i - 1)
                    elif not first:
                        reciprocals(P * NT - 1, P * STEPS - 1, NT - 1)
                    row_max(P * STEPS + 2 * i + 1, i, 1)
                    if i > 0:
                        replicate(P * NT + i - 1, i - 1)
                    elif not first:
                        replicate(P * NT - 1, NT - 1)
                    if yb is not None and i > 0:
                        output(yb, i - 1, pO[:, 2 * P128:])
                    if i == 0 and not first:
                        values(P * NT - 1, PAIRS - 1 if yb is not None else p - 1, NT - 1)
                    if not last:
                        if not first or i >= 2:
                            dve.wait_ge(rot_done, (P + 1) * NT + i - 1)
                        rope((P + 1) * NT + i, i, 1 - par, pP)
                    if i > 0:
                        values(P * NT + i - 1, p, i - 1)
                    if yb is not None:
                        rest(yb, i)
                    if i + 1 < NT:
                        row_max(P * STEPS + 2 * i + 2, i + 1, 0)
                    elif not last:
                        row_max(P * STEPS + STEPS, 0, 0)
                    if i == 0:
                        stack(P * NT + NT - 1, NT - 1, par)
                    elif not last:
                        stack((P + 1) * NT + i - 1, i - 1, 1 - par)
                if yb is not None:
                    output(yb, NT - 1, pO[:, 2 * P128:])

            def tail():
                reciprocals(LAST * NT + NT - 1, LAST * STEPS + STEPS - 1, NT - 1)
                replicate(LAST * NT + NT - 1, NT - 1)
                values(LAST * NT + NT - 1, PAIRS - 1, NT - 1)
                rest(B - 1, 0)
                for t in range(NT):
                    if t + 1 < NT:
                        rest(B - 1, t + 1)
                    output(B - 1, t, pT[t % 2][:, 0:C])

            prologue()
            pairs(dve, attend)
            tail()

        @block.tensor
        def _(pe):
            pe.wait_ge(const_made, 4)
            pe.wait_ge(identr_made, 2)
            pe.wait_ge(wo_loaded, 16)

            def project(TI, t, par, bank):
                n = 0
                for k in range(KT):
                    for hx, hw in ((0, 0), (0, 1), (1, 0)):
                        mm = pe.matmul(bank[:, 0:QKV], xT[:, t, hx, k, :], w[:, par, hw, k, :],
                                       start=(n == 0), stop=(n == 3 * KT - 1))
                        n += 1
                mm.then_inc(proj_done, 1)

            def stack(TI, t, more):
                u = t % 2
                if more:
                    pe.wait_ge(rope_done, TI + 2)
                pe.wait_ge(rot_done, TI + 1)
                for h in range(2):
                    pe.transpose(pP[:, h * P128:(h + 1) * P128], rq[:, u, h, :, :].rearrange("p a d -> p (a d)"), ident[:, :])
                for h in range(2):
                    mm = pe.matmul(pP[:, (2 + h) * P128:(3 + h) * P128], kk[:, u, h, :, :].rearrange("p a d -> p (a d)"),
                                   identr[:, :], start=True, stop=True)
                mm.then_inc(stackT_done, 1)

            def scores(TI, SI, i, h, par, fresh):
                s = (2 * i + h) % 2
                pe.wait_ge(stack_lo, TI + 1)
                if not fresh:
                    pe.wait_ge(exp_done, SI - 1)
                width = (i + 1) * P128
                q = slice(i * P128, (i + 1) * P128)
                for c0 in range(0, width, BANK):
                    c1 = min(c0 + BANK, width)
                    diag = c1 == width
                    pe.matmul(pS[s][:, c0:c1], QH[:, par, h, q], KS[:, par, h, c0:c1], start=True, stop=False)
                    mm = pe.matmul(pS[s][:, c0:c1], QL[:, par, h, q], KS[:, par, h, c0:c1], start=False, stop=not diag)
                mm = pe.matmul(pS[s][:, width - P128:width], identb[:, :], maskb[:, :], start=False, stop=True)
                mm.then_inc(s_done, 1)

            def transposes(P, SI, i, h, lag):
                s = (2 * i + h) % 2
                pe.wait_ge(exp_done, SI + 1)
                for c in range(CH[i]):
                    n = chunk0(i, h) + c
                    if lag or n >= 2:
                        pe.wait_ge(evac_done, P * CHUNKS + n - 1)
                    for j in range(4 * c, min(4 * c + 4, i + 1)):
                        tr = pe.transpose(pT[n % 2][:, (j - 4 * c) * P128:(j - 4 * c + 1) * P128],
                                          Pr[:, s, j * P128:(j + 1) * P128], ident[:, :])
                    tr.then_inc(t_done, 1)

            def values(P, OI, i, par):
                pe.wait_ge(rep_done, OI + 1)
                pe.wait_ge(o_done, OI)
                pe.transpose(pO[:, P128:2 * P128], rep[:, i % 2, :, :].rearrange("p h d -> p (h d)"), ident[:, :])
                pe.wait_ge(evac_done, P * CHUNKS + chunk0(i, 1) + CH[i])
                for j in range(i + 1):
                    for h in range(2):
                        mm = pe.matmul(pO[h * DH:(h + 1) * DH, 0:P128], V[:, par, j, h * DH:(h + 1) * DH],
                                       PT[:, i % 2, h, j * P128:(j + 1) * P128], start=(j == 0), stop=(j == i))
                mm.then_inc(pv_done, 1)

            def output(y, t, bank):
                u = t % 2
                pe.matmul(bank, wsp[:, t * P128:(t + 1) * P128], oe[:, :], start=True, stop=False)
                pe.wait_ge(ol_done, y * NT + t + 1)
                n = 0
                for k in range(PAIRS):
                    for o, hw in ((oh, 0), (oh, 1), (ol, 0)):
                        n += 1
                        mm = pe.matmul(bank, o[:, u, k, :], wo[:, hw, k, :], start=False, stop=(n == 3 * PAIRS))
                mm.then_inc(y_mm, 1)

            def prologue():
                pe.wait_ge(w_loaded[0], 16)
                for t in range(NT):
                    pe.wait_ge(xt_loaded[t], 16)
                    if t >= 4:
                        pe.wait_ge(rope_done, t - 3)
                    project(t, t, 0, first_bank(t))
                    if t >= 2:
                        if t >= 3:
                            pe.wait_ge(stack_lo, t - 2)
                        stack(t - 2, t - 2, False)
                pe.wait_ge(stack_lo, NT - 2)
                stack(NT - 2, NT - 2, False)
                pe.wait_ge(rope_done, NT)
                scores(0, 0, 0, 0, 0, True)

            def attend(P, p, par, first, last, yb, crossing):
                if not last:
                    pe.wait_ge(w_loaded[1 - par], 16 if first else (P + 2 + par) * 8)
                for i in range(NT):
                    SI = P * STEPS + 2 * i
                    scores(P * NT + i, SI + 1, i, 1, par, first and i == 0)
                    if not last:
                        TI = (P + 1) * NT + i
                        if crossing is not None:
                            pe.wait_ge(xt_loaded[i], (crossing + 2) * 16)
                        pe.wait_ge(stack_lo, TI - 1)
                        project(TI, i, 1 - par, pP)
                    transposes(P, SI, i, 0, not first)
                    if i > 0:
                        if yb is not None:
                            pe.wait_ge(y_done, yb * NT + i)
                        values(P, P * NT + i - 1, i - 1, par)
                    elif not first:
                        values(P - 1, P * NT - 1, NT - 1, 1 - par)
                    if i + 1 < NT:
                        scores(P * NT + i + 1, SI + 2, i + 1, 0, par, False)
                    elif not last:
                        scores((P + 1) * NT, SI + 2, 0, 0, 1 - par, False)
                    if i == 0:
                        stack(P * NT + NT - 1, NT - 1, not last)
                    elif not last:
                        stack((P + 1) * NT + i - 1, i - 1, True)
                    transposes(P, SI + 1, i, 1, not first)
                    if yb is not None:
                        if i == 0:
                            pe.wait_ge(moe_loaded, (yb + 1) * 32)
                        pe.wait_ge(o_done, P * NT + i)
                        output(yb, i, pO[:, 2 * P128:])
                if yb is not None:
                    pe.wait_ge(y_done, (yb + 1) * NT)

            def tail():
                values(LAST, LAST * NT + NT - 1, NT - 1, 1)
                pe.wait_ge(moe_loaded, B * 32)
                pe.wait_ge(evac_done, B * PAIRS * CHUNKS)
                for t in range(NT):
                    if t >= 2:
                        pe.wait_ge(y_done, (B - 1) * NT + t - 1)
                    output(B - 1, t, pT[t % 2][:, 0:C])

            prologue()
            pairs(pe, attend)
            tail()


def build(nc, x, wq, wk, wv, wo, bo, gate_w, gate_b, w1, w2, rot_cos, rot_sin, out):
    def dram(name, shape):
        return nc.dram_tensor(name, shape, F32, kind="Internal").ap()

    xt_s = dram("xt_s", (B, P128, 2, KT, T))
    xn_s = dram("xn_s", (B, P128, NT, C))
    w_s = dram("w_s", (PAIRS, P128, 2, KT, QKV))
    wo_s = dram("wo_s", (P128, 2, PAIRS, C))
    logit_s = dram("logit_s", (B, E, T))
    wsp_s = dram("wsp_s", (B, E, T))
    mgt_s = dram("mgt_s", (P128, KT, P128))
    o_s = dram("o_s", (B, E, C))
    prepare_block(nc, x, wq, wk, wv, wo, gate_w, gate_b, xt_s, w_s, wo_s, logit_s, xn_s)
    route_block(nc, logit_s, xn_s, wsp_s, mgt_s)
    experts_block(nc, w1, w2, mgt_s, o_s)
    attend_block(nc, x, bo, rot_cos, rot_sin, xt_s, w_s, wo_s, wsp_s, o_s, out)


_INS = ["L0_attn_x", "L0_attn_Wq", "L0_attn_Wk", "L0_attn_Wv", "L0_attn_Wo", "L0_attn_bo",
        "L0_ffn_gate_w", "L0_ffn_gate_b", "L0_ffn_w1", "L0_ffn_w2"]


def rotation_tables():
    import numpy as np
    inv = (1.0 / 10000.0 ** (np.arange(0, DH, 2, dtype=np.float32) / np.float32(DH))).astype(np.float32)
    ang = (np.arange(T, dtype=np.float32)[:, None] * inv[None, :]).astype(np.float32)
    cos = np.repeat(np.cos(ang), 2, axis=1)
    sin = np.stack([-np.sin(ang), np.sin(ang)], axis=-1).reshape(T, DH)
    return np.ascontiguousarray(cos, dtype=np.float32), np.ascontiguousarray(sin, dtype=np.float32)


def kernel(**inputs):
    import numpy as _np
    import concourse.bacc as _bacc
    from concourse import mybir as _mybir
    from concourse.bass_utils import run_bass_kernel_spmd as _run

    nc = _bacc.Bacc("TRN2", target_bir_lowering=False, num_devices=1)
    cos, sin = rotation_tables()
    arrays, args = {}, []
    for name, a in [(n, inputs[n]) for n in _INS] + [("rot_cos", cos), ("rot_sin", sin)]:
        a = _np.ascontiguousarray(a)
        arrays[f"in_{name}"] = a
        args.append(nc.dram_tensor(f"in_{name}", a.shape, _mybir.dt.from_np(a.dtype), kind="ExternalInput").ap())
    args.append(nc.dram_tensor("out_0", (B, T, C), F32, kind="ExternalOutput").ap())
    build(nc, *args)
    r = _run(nc, [arrays], core_ids=[0])
    return r.results[0]["out_0"]
```

```python
from contextlib import ExitStack

import concourse.bass as bass
from concourse import mybir

F32 = mybir.dt.float32
F32R = mybir.dt.float32r
BF16 = mybir.dt.bfloat16
ALU = mybir.AluOpType
ACT = mybir.ActivationFunctionType
AX_X = mybir.AxisListType.X

B, T, C = 4, 1024, 256
HEADS, DH = 16, 64
INNER = HEADS * DH
E, TOPK, HID = 32, 8, 1024
P128 = 128
NT = T // P128
KT = C // P128
PAIRS = HEADS // 2
QKV = 3 * P128
BANK = 512
SCALE = DH ** -0.5
EPS = 1e-5
MASKED = -1.0e30
USED = -3.0e38
Q4 = HID // 4
GE = 4


def build_identity(pool, ap, sem, base):
    pool.memset(ap, 0.0).then_inc(sem, 1)
    pool.wait_ge(sem, base + 1)
    pool.affine_select(out=ap, in_=ap, compare_op=ALU.not_equal, fill=1.0, base=0,
                       pattern=[[-1, ap.shape[-1]]], channel_multiplier=1).then_inc(sem, 1)


def load_weights(q, wraw, wq, wk, wv, p, sem):
    for n, w in enumerate((wq, wk, wv)):
        q.dma_start(wraw[:, :, n * P128:(n + 1) * P128],
                    w[:, bass.ds(p * P128, P128)].rearrange("(k p) n -> p k n", p=P128)).then_inc(sem, 16)


def prepare_block(nc, x, gate_w, gate_b, wq, wk, wv, wo, woraw, xt_s, L, xn, w, wraw, wscaled, wscale, consts):
    ident, identr, identb, maskb = consts
    with ExitStack() as ctx:
        def sb(name, shape, dt=F32):
            return ctx.enter_context(nc.sbuf_tensor(name, shape, dt))

        def ps(name, shape):
            return ctx.enter_context(nc.psum_tensor(name, shape, F32))

        def sem(name):
            return ctx.enter_context(nc.semaphore(name))

        gw = sb("a_gw", [E, C])
        gb = sb("a_gb", [P128, 1])
        gT = sb("a_gT", [P128, B, KT, P128])
        gThl = sb("a_gThl", [P128, 2, B, KT, P128], F32R)
        xin = sb("a_xin", [P128, B, NT, C])
        stats = sb("a_stats", [P128, NT, 6])
        both = sb("a_both", [P128, NT])
        gap = sb("a_gap", [P128, NT])
        gap2 = sb("a_gap2", [P128, NT])
        square = sb("a_square", [P128, NT])
        mse = sb("a_mse", [P128, NT])
        mean = sb("a_mean", [P128, 2, NT])
        ve = sb("a_ve", [P128, NT])
        sd = sb("a_sd", [P128, NT])
        r0 = sb("a_r0", [P128, NT])
        r1 = sb("a_r1", [P128, NT])
        r2 = sb("a_r2", [P128, NT])
        r3 = sb("a_r3", [P128, NT])
        rstd = sb("a_rstd", [P128, 2, NT])
        xThl = sb("a_xThl", [P128, 2, 2, KT, T], F32R)
        pT = ps("a_pT", [P128, KT, T])
        pL = ps("a_pL", [P128, T])
        pG = ps("a_pG", [P128, BANK])

        g_loaded = sem("a_g_loaded")
        wo_loaded = sem("a_wo_loaded")
        gb_loaded = sem("a_gb_loaded")
        x_loaded = [sem(f"a_x_loaded{b}") for b in range(B)]
        ident_made = sem("a_ident_made")
        g_trans = sem("a_g_trans")
        g_zero = sem("a_g_zero")
        g_copied = sem("a_g_copied")
        g_hi = sem("a_g_hi")
        g_lo = sem("a_g_lo")
        stat_done = sem("a_stat_done")
        sqrt_done = sem("a_sqrt_done")
        xn_done = sem("a_xn_done")
        xn_done2 = sem("a_xn_done2")
        mask_made = sem("a_mask_made")
        scale_made = sem("a_scale_made")
        w_loaded = sem("a_w_loaded")
        w_scaled = sem("a_w_scaled")
        w_split = sem("a_w_split")
        xt_done = sem("a_xt_done")
        xt_hi = sem("a_xt_hi")
        xt_lo = sem("a_xt_lo")
        logit_done = sem("a_logit_done")
        xt_stored = [sem(f"a_xt_stored{i}") for i in range(2)]
        STAT = 9
        OURS = 7

        block = ctx.enter_context(nc.Block())

        @block.sync
        def _(sp):
            for b in range(B):
                sp.dma_start(xin[:, b, :, :], x[b, :, :].rearrange("(t p) c -> p t c", p=P128)).then_inc(x_loaded[b], 16)
            for b in range(B):
                for half, made in ((0, xt_hi), (1, xt_lo)):
                    for k in range(KT):
                        sp.wait_ge(made, b * KT + k + 1)
                        sp.dma_start(xt_s[b, :, :, half, k, :],
                                     xThl[:, b % 2, half, k, :].rearrange("p (t n) -> p t n", n=P128).bitcast(F32)
                                     ).then_inc(xt_stored[b % 2], 16)
            for u in range(2):
                sp.wait_ge(xt_stored[u], B // 2 * 64)

        @block.scalar
        def _(act):
            act.dma_start(gw[:, :], gate_w).then_inc(g_loaded, 16)
            for b in range(B):
                act.dma_start(gb[b * E:(b + 1) * E, :], gate_b.rearrange("(e a) -> e a", a=1)).then_inc(gb_loaded, 16)

            def sqrt(b):
                act.wait_ge(stat_done, b * STAT + 4)
                act.activation(sd[:, :], ve[:, :], ACT.Sqrt).then_inc(sqrt_done, 1)

            load_weights(act, wraw, wq, wk, wv, 0, w_loaded)
            sqrt(0)
            for b in range(B):
                if b == 1:
                    act.wait_ge(w_scaled, 1)
                    load_weights(act, wraw, wq, wk, wv, 1, w_loaded)
                if b == B - 1:
                    act.dma_start(woraw[:, :, :], wo.rearrange("(k p) n -> p k n", p=P128)).then_inc(wo_loaded, 16)
                if b + 1 < B:
                    sqrt(b + 1)
                if b >= 2:
                    act.wait_ge(xt_stored[b % 2], (b // 2) * 64)
                for k in range(KT):
                    act.wait_ge(xt_done, b * KT + k + 1)
                    act.activation(xThl[:, b % 2, 0, k, :], pT[:, k, :], ACT.Copy).then_inc(xt_hi, 1)
            act.wait_ge(wo_loaded, 16)
            act.wait_ge(gb_loaded, B * 16)
            act.wait_ge(logit_done, B)
            act.activation(L[:, :], pL[:, :], ACT.Identity, bias=gb[:, :])

        @block.gpsimd
        def _(pool):
            build_identity(pool, ident[:, :], ident_made, 0)
            pool.memset(gT[:, :, :, :], 0.0).then_inc(g_zero, 1)
            pool.memset(wscale[:, 0:P128], SCALE).then_inc(scale_made, 1)
            pool.memset(wscale[:, P128:], 1.0).then_inc(scale_made, 1)
            pool.memset(maskb[:, :], 0.0).then_inc(mask_made, 1)
            pool.wait_ge(mask_made, 1)
            pool.affine_select(out=maskb[:, :], in_=maskb[:, :], compare_op=ALU.is_ge, fill=MASKED, base=0,
                               pattern=[[-1, P128]], channel_multiplier=1)
            pool.wait_ge(ident_made, 2)
            pool.tensor_copy(identr[:, :], ident[:, :])
            pool.tensor_copy(identb[:, :], ident[:, :])
            pool.wait_ge(scale_made, 2)
            for b in range(B):
                u = b % 2
                pool.wait_ge(stat_done, (b + 1) * STAT)
                for t in range(OURS, NT):
                    pool.tensor_scalar(xn[:, b, t, :], xin[:, b, t, :], mean[:, u, t:t + 1], rstd[:, u, t:t + 1],
                                       ALU.subtract, ALU.mult).then_inc(xn_done2, 1)
                if b < 2:
                    pool.wait_ge(w_loaded, (b + 1) * 48)
                    if b > 0:
                        pool.wait_ge(w_split, b)
                    sv = wscale[:, :].unsqueeze(1).to_broadcast([P128, KT, QKV])
                    pool.tensor_tensor(w[:, b, 0, :, :], wraw[:, :, :], sv, ALU.mult)
                    pool.tensor_tensor(wscaled[:, :, :], wraw[:, :, :], sv, ALU.mult).then_inc(w_scaled, 1)
                    pool.wait_ge(w_scaled, b + 1)
                    pool.tensor_tensor(w[:, b, 1, :, :], wscaled[:, :, :], w[:, b, 0, :, :].bitcast(F32),
                                       ALU.subtract).then_inc(w_split, 1)

        @block.vector
        def _(dve):
            def gate():
                dve.wait_ge(g_trans, 1)
                dve.wait_ge(g_zero, 1)
                for b in range(B):
                    dve.tensor_copy(gT[:, b, :, b * E:(b + 1) * E],
                                    pG[:, 0:KT * E].rearrange("p (k e) -> p k e", k=KT)).then_inc(g_copied, 1)
                dve.wait_ge(g_copied, B)
                dve.tensor_copy(gThl[:, 0, :, :, :], gT[:, :, :, :]).then_inc(g_hi, 1)
                dve.wait_ge(g_hi, 1)
                dve.tensor_tensor(gThl[:, 1, :, :, :], gT[:, :, :, :], gThl[:, 0, :, :, :].bitcast(F32), ALU.subtract).then_inc(g_lo, 1)

            def normalise(b):
                u = b % 2
                dve.wait_ge(x_loaded[b], 16)
                for t in range(NT):
                    st = dve.bn_stats(stats[:, t, :], xin[:, b, t, :])
                st.then_inc(stat_done, 1)
                dve.wait_ge(stat_done, b * STAT + 1)
                dve.tensor_tensor(both[:, :], stats[:, :, 1], stats[:, :, 4], ALU.add)
                dve.tensor_tensor(gap[:, :], stats[:, :, 1], stats[:, :, 4], ALU.subtract)
                dve.tensor_tensor(square[:, :], stats[:, :, 2], stats[:, :, 5], ALU.add).then_inc(stat_done, 1)
                dve.wait_ge(stat_done, b * STAT + 2)
                if b >= 2:
                    dve.wait_ge(xn_done2, (b - 1) * (NT - OURS))
                dve.tensor_scalar(mean[:, u, :], both[:, :], 0.5, None, ALU.mult)
                dve.tensor_tensor(gap2[:, :], gap[:, :], gap[:, :], ALU.mult)
                dve.tensor_scalar(mse[:, :], square[:, :], 1.0 / C, EPS, ALU.mult, ALU.add).then_inc(stat_done, 1)
                dve.wait_ge(stat_done, b * STAT + 3)
                dve.scalar_tensor_tensor(ve[:, :], gap2[:, :], 0.25, mse[:, :], ALU.mult, ALU.add).then_inc(stat_done, 1)
                dve.wait_ge(sqrt_done, b + 1)
                dve.reciprocal(r0[:, :], sd[:, :]).then_inc(stat_done, 1)
                dve.wait_ge(stat_done, b * STAT + 5)
                dve.tensor_tensor(r1[:, :], r0[:, :], r0[:, :], ALU.mult).then_inc(stat_done, 1)
                dve.wait_ge(stat_done, b * STAT + 6)
                dve.tensor_tensor(r2[:, :], r1[:, :], ve[:, :], ALU.mult).then_inc(stat_done, 1)
                dve.wait_ge(stat_done, b * STAT + 7)
                dve.tensor_scalar(r3[:, :], r2[:, :], -0.5, 1.5, ALU.mult, ALU.add).then_inc(stat_done, 1)
                dve.wait_ge(stat_done, b * STAT + 8)
                dve.tensor_tensor(rstd[:, u, :], r3[:, :], r0[:, :], ALU.mult).then_inc(stat_done, 1)
                dve.wait_ge(stat_done, b * STAT + 9)
                for t in range(OURS):
                    dve.tensor_scalar(xn[:, b, t, :], xin[:, b, t, :], mean[:, u, t:t + 1], rstd[:, u, t:t + 1],
                                      ALU.subtract, ALU.mult).then_inc(xn_done, 1)

            normalise(0)
            gate()
            for b in range(B):
                if b + 1 < B:
                    normalise(b + 1)
                for k in range(KT):
                    dve.wait_ge(xt_hi, b * KT + k + 1)
                    if b >= 2:
                        dve.wait_ge(xt_stored[b % 2], (b // 2) * 64)
                    dve.tensor_tensor(xThl[:, b % 2, 1, k, :], pT[:, k, :], xThl[:, b % 2, 0, k, :].bitcast(F32),
                                      ALU.subtract).then_inc(xt_lo, 1)

        @block.tensor
        def _(pe):
            pe.wait_ge(ident_made, 2)
            pe.wait_ge(g_loaded, 16)
            for k in range(KT):
                tr = pe.transpose(pG[:, k * E:(k + 1) * E], gw[:, k * P128:(k + 1) * P128], ident[0:E, 0:E])
            tr.then_inc(g_trans, 1)
            for b in range(B):
                for k in range(KT):
                    if b >= 1:
                        pe.wait_ge(xt_lo, (b - 1) * KT + k + 1)
                    for t in range(NT):
                        if t < OURS:
                            pe.wait_ge(xn_done, b * OURS + t + 1)
                        else:
                            pe.wait_ge(xn_done2, b * (NT - OURS) + t - OURS + 1)
                        tr = pe.transpose(pT[:, k, t * P128:(t + 1) * P128], xn[:, b, t, k * P128:(k + 1) * P128], ident[:, :])
                    tr.then_inc(xt_done, 1)
                pe.wait_ge(xt_lo, (b + 1) * KT)
                pe.wait_ge(g_lo, 1)
                for c in range(T // BANK):
                    n = 0
                    for k in range(KT):
                        for hg, hx in ((0, 0), (0, 1), (1, 0)):
                            mm = pe.matmul(pL[:, c * BANK:(c + 1) * BANK], gThl[:, hg, b, k, :],
                                           xThl[:, b % 2, hx, k, c * BANK:(c + 1) * BANK],
                                           start=(b == 0 and n == 0), stop=(b == B - 1 and n == 3 * KT - 1))
                            n += 1
                mm.then_inc(logit_done, 1)


def route_block(nc, woraw, rot_cos, rot_sin, L, xt_s, wsp_s, wo_s, xn, mgT, xT, cos, sin, ident, bo, mT, b1, b2, bob):
    with ExitStack() as ctx:
        def sb(name, shape, dt=F32):
            return ctx.enter_context(nc.sbuf_tensor(name, shape, dt))

        def ps(name, shape):
            return ctx.enter_context(nc.psum_tensor(name, shape, F32))

        def sem(name):
            return ctx.enter_context(nc.semaphore(name))

        Lr = sb("r_Lr", [P128, T])
        Ex = sb("r_Ex", [P128, T])
        taken = sb("r_taken", [P128, T])
        W = sb("r_W", [P128, T])
        WT = sb("r_WT", [P128, NT, P128])
        wohl = sb("r_wohl", [P128, 2, PAIRS, C], F32R)
        top = sb("r_top", [P128, 8])
        nmax = sb("r_nmax", [P128, 1])
        total = sb("r_total", [P128, 1])
        rtotal = sb("r_rtotal", [P128, 1])
        mg = sb("r_mg", [P128, C])
        pW = ps("r_pW", [P128, T])
        pM = ps("r_pM", [P128, BANK])
        pMT = ps("r_pMT", [P128, BANK])

        xt_loaded = sem("r_xt_loaded")
        bo_loaded = sem("r_bo_loaded")
        table_loaded = sem("r_table_loaded")
        wo_hi = sem("r_wo_hi")
        wo_lo = sem("r_wo_lo")
        wo_stored = sem("r_wo_stored")
        dv = sem("r_dv")
        ex_done = sem("r_ex_done")
        wt_done = sem("r_wt_done")
        wt_copied = sem("r_wt_copied")
        mg_done = sem("r_mg_done")
        mgt_done = sem("r_mgt_done")
        stored = sem("r_stored")
        block = ctx.enter_context(nc.Block())

        @block.sync
        def _(sp):
            sp.dma_start(xT[:, :, :, :, :].bitcast(F32), xt_s[0]).then_inc(xt_loaded, 16)
            sp.wait_ge(dv, 6)
            sp.dma_start(wsp_s.rearrange("b e t -> (b e) t"), W[:, :]).then_inc(stored, 16)
            sp.wait_ge(stored, 16)
            sp.wait_ge(xt_loaded, 16)

        @block.gpsimd
        def _(pool):
            pool.memset(mgT[:, :, :, E:], 0.0)
            pool.memset(mT[:, :, :, :], 0.0)
            pool.memset(b1[:, :, :], 0.0)
            pool.memset(b2[:, :, :], 0.0)
            pool.dma_start(bob[:, :], bo.rearrange("(a n) -> a n", a=1).to_broadcast([P128, C])).then_inc(bo_loaded, 16)
            pool.wait_ge(bo_loaded, 16)

        @block.scalar
        def _(act):
            act.activation(wohl[:, 0, :, :], woraw[:, :, :], ACT.Copy).then_inc(wo_hi, 1)
            act.dma_start(cos[:, :, :], rot_cos.rearrange("(t p) d -> p t d", p=P128)).then_inc(table_loaded, 16)
            act.dma_start(sin[:, :, :], rot_sin.rearrange("(t p) d -> p t d", p=P128)).then_inc(table_loaded, 16)
            act.wait_ge(dv, 2)
            act.activation(Ex[:, :], L[:, :], ACT.Exp, bias=nmax[:, :], accum_out=total[:, :]).then_inc(ex_done, 1)
            act.wait_ge(wt_done, 1)
            act.activation(WT[:, :, :].rearrange("p t m -> p (t m)"), pW[:, :], ACT.Copy).then_inc(wt_copied, 1)
            for half, made in ((0, wo_hi), (1, wo_lo)):
                act.wait_ge(made, 1)
                act.dma_start(wo_s[:, half, :, :], wohl[:, half, :, :].bitcast(F32)).then_inc(wo_stored, 16)
            act.wait_ge(wo_stored, 32)
            act.wait_ge(table_loaded, 32)

        @block.vector
        def _(dve):
            dve.max(top[:, :], L[:, :]).then_inc(dv, 1)
            dve.wait_ge(dv, 1)
            dve.tensor_scalar(nmax[:, :], top[:, 0:1], -1.0, None, ALU.mult).then_inc(dv, 1)
            dve.match_replace(out=Lr[:, :], in_to_replace=top[:, :], in_values=L[:, :], imm_value=USED).then_inc(dv, 1)
            dve.wait_ge(dv, 3)
            dve.tensor_tensor(taken[:, :], Lr[:, :], L[:, :], ALU.not_equal).then_inc(dv, 1)
            dve.wait_ge(ex_done, 1)
            dve.reciprocal(rtotal[:, :], total[:, :]).then_inc(dv, 1)
            dve.wait_ge(dv, 5)
            dve.scalar_tensor_tensor(W[:, :], Ex[:, :], rtotal[:, :], taken[:, :], ALU.mult, ALU.mult).then_inc(dv, 1)
            dve.wait_ge(wo_hi, 1)
            dve.tensor_tensor(wohl[:, 1, :, :], woraw[:, :, :], wohl[:, 0, :, :].bitcast(F32), ALU.subtract).then_inc(wo_lo, 1)
            dve.wait_ge(mg_done, 1)
            dve.tensor_copy(mg[:, :], pM[:, 0:C]).then_inc(dv, 1)
            dve.wait_ge(mgt_done, 1)
            dve.tensor_copy(mgT[:, :, :, 0:E], pMT[:, 0:KT * P128].rearrange("p (k b e) -> p k b e", k=KT, b=B)).then_inc(dv, 1)

        @block.tensor
        def _(pe):
            pe.wait_ge(dv, 6)
            for t in range(NT):
                tr = pe.transpose(pW[:, t * P128:(t + 1) * P128], W[:, t * P128:(t + 1) * P128], ident[:, :])
            tr.then_inc(wt_done, 1)
            pe.wait_ge(wt_copied, 1)
            for t in range(NT):
                for b in range(B):
                    mm = pe.matmul(pM[b * E:(b + 1) * E, 0:C], WT[:, t, b * E:(b + 1) * E], xn[:, b, t, :],
                                   start=(t == 0), stop=(t == NT - 1))
            mm.then_inc(mg_done, 1)
            pe.wait_ge(dv, 7)
            for k in range(KT):
                tr = pe.transpose(pMT[:, k * P128:(k + 1) * P128], mg[:, k * P128:(k + 1) * P128], ident[:, :])
            tr.then_inc(mgt_done, 1)


def attend_block(nc, x, wq, wk, wv, w1, w2, xt_s, wo_s, wsp_s, o_s, mgT, xT, w, wraw, wscaled, wscale, cos, sin, consts, mT, b1, b2, bob, out):
    CH = [(i + 4) // 4 for i in range(NT)]
    CHUNKS = 2 * sum(CH)
    STEPS = 2 * NT
    ident, identr, identb, maskb = consts

    def chunk0(i, h):
        return 2 * sum(CH[:i]) + h * CH[i]

    FULL = [(0, False, "turn", 0), (1, False, "layer2", 0), (2, False, "layer1", 0), (3, False, "turn", 1),
            (4, True, "layer2", 1), (4, False, "layer1", 1), (5, True, "turn", 2), (5, False, "layer2", 2),
            (6, True, "layer1", 2), (6, False, "turn", 3), (7, True, "layer1", 3), (7, False, "layer2", 3)]
    FINAL = [s for s in FULL if s[2] != "layer1"]

    def slots_of(G, final):
        return [(s, GE + G * len(FULL) + n) for n, s in enumerate(FINAL if final else FULL)]

    def slots_at(G, final, i, before):
        return [] if G is None else [(s[2], s[3], n) for s, n in slots_of(G, final) if s[0] == i and s[1] == before]

    def slot_count(G, final, kind, k):
        return [n + 1 for s, n in slots_of(G, final) if s[2] == kind and s[3] == k][0]

    with ExitStack() as ctx:
        def sb(name, shape, dt=F32):
            return ctx.enter_context(nc.sbuf_tensor(name, shape, dt))

        def ps(name, shape):
            return ctx.enter_context(nc.psum_tensor(name, shape, F32))

        def sem(name):
            return ctx.enter_context(nc.semaphore(name))

        with nc.sbuf_tensor("t_w1t", [P128, 2, KT, HID], F32) as w1t, nc.sbuf_tensor("t_w2t", [P128, 2, 4, 2, C], F32) as w2t:
            pass
        wo = sb("t_wo", [P128, 2, PAIRS, C], F32R)
        oh = sb("t_oh", [P128, 2, PAIRS, P128], F32R)
        ol = sb("t_ol", [P128, 2, PAIRS, P128], F32R)
        QH = sb("t_QH", [P128, 2, T], F32R)
        QL = sb("t_QL", [P128, 2, T], F32R)
        KS = sb("t_KS", [P128, 2, 2, T], F32R)
        V = sb("t_V", [P128, 2, NT, P128])
        rc = sb("t_rc", [P128, 2, 2 * P128])
        rs = sb("t_rs", [P128, 2, 2 * P128])
        rq = sb("t_rq", [P128, 2, 2, 2, DH])
        rk = sb("t_rk", [P128, 2, 2, DH])
        kk = sb("t_kk", [P128, 2, 2, 2, DH], F32R)
        nmax = sb("t_nmax", [P128, 2])
        psum_row = sb("t_sum", [P128, 2, 2])
        recip = sb("t_recip", [P128, 2, 2])
        rep = sb("t_rep", [P128, 2, 2, DH])
        Pr = sb("t_Pr", [P128, 2, T])
        PT = sb("t_PT", [P128, 2, 2, T])
        rT = sb("t_rT", [P128, P128])
        OT = sb("t_OT", [P128, PAIRS, T])
        wsp = sb("t_wsp", [P128, T])
        oe = sb("t_oe", [P128, C])
        with nc.sbuf_tensor("t_part", [P128, GE, C], F32) as part:
            pass
        xin = sb("t_xin", [P128, 2, C])
        xb = sb("t_xb", [P128, 2, C])
        yt = sb("t_yt", [P128, 2, C])
        g = sb("t_g", [P128, GE, Q4])
        hT = sb("t_hT", [P128, 2, P128])
        pS = [ps(f"t_pS{i}", [P128, T]) for i in range(2)]
        pT = [ps(f"t_pT{i}", [P128, BANK]) for i in range(2)]
        pO = ps("t_pO", [P128, BANK])
        pP = ps("t_pP", [P128, BANK])

        wo_loaded = sem("t_wo_loaded")
        xt_loaded = [sem(f"t_xt_loaded{t}") for t in range(NT)]
        wraw_loaded = sem("t_wraw_loaded")
        w_scaled = sem("t_w_scaled")
        w_lo = sem("t_w_lo")
        recip_done = sem("t_recip_done")
        moe_loaded = sem("t_moe_loaded")
        w1_loaded = [sem(f"t_w1_loaded{i}") for i in range(2)]
        w2_loaded = [sem(f"t_w2_loaded{i}") for i in range(2)]
        b1_loaded = sem("t_b1_loaded")
        b2_loaded = sem("t_b2_loaded")
        mT_done = sem("t_mT_done")
        g_done = sem("t_g_done")
        slot_done = sem("t_slot_done")
        slot_read = sem("t_slot_read")
        part_stored = sem("t_part_stored")
        x_loaded = [sem(f"t_x_loaded{i}") for i in range(2)]
        proj_done = sem("t_proj_done")
        rope_done = sem("t_rope_done")
        rk_done = sem("t_rk_done")
        kh_done = sem("t_kh_done")
        rot_done = sem("t_rot_done")
        stackT_done = sem("t_stackT_done")
        stack_hi = sem("t_stack_hi")
        stack_lo = sem("t_stack_lo")
        s_done = sem("t_s_done")
        max_done = sem("t_max_done")
        exp_done = sem("t_exp_done")
        t_done = sem("t_t_done")
        evac_done = sem("t_evac_done")
        rep_done = sem("t_rep_done")
        pv_done = sem("t_pv_done")
        rt_copied = sem("t_rt_copied")
        o_done = sem("t_o_done")
        oh_done = sem("t_oh_done")
        ol_done = sem("t_ol_done")
        xb_done = sem("t_xb_done")
        y_mm = sem("t_y_mm")
        y_done = sem("t_y_done")
        y_stored = [sem(f"t_y_stored{i}") for i in range(2)]
        block = ctx.enter_context(nc.Block())

        LAST = B * PAIRS - 1

        def first_bank(t):
            return pS[t // 2 % 2][:, t % 2 * BANK:(t % 2 + 1) * BANK]

        def first_stack(t):
            return (pP, pO)[t % 2][:, :]

        def stack_bank(i):
            return pS[1][:, BANK:] if i < 3 else pP[:, :]

        def pairs(engine, attend):
            attend(0, 0, 0, first=True, group=0)
            with engine.Fori(0, PAIRS // 2 - 1) as g:
                attend(g * 2 + 1, g * 2 + 1, 1, group=g * 2 + 1)
                attend(g * 2 + 2, g * 2 + 2, 0, group=g * 2 + 2)
            attend(PAIRS - 1, PAIRS - 1, 1, crossing=0, group=PAIRS - 1, final=True)
            attend(PAIRS, 0, 0, yb=0, late=True)
            with engine.Fori(1, B - 1) as b:
                with engine.Fori(0, PAIRS // 2 - 1) as g:
                    attend(b * PAIRS + g * 2 + 1, g * 2 + 1, 1)
                    attend(b * PAIRS + g * 2 + 2, g * 2 + 2, 0)
                attend(b * PAIRS + PAIRS - 1, PAIRS - 1, 1, crossing=b)
                attend(b * PAIRS + PAIRS, 0, 0, yb=b)
            with engine.Fori(0, PAIRS // 2 - 1) as g:
                attend((B - 1) * PAIRS + g * 2 + 1, g * 2 + 1, 1)
                attend((B - 1) * PAIRS + g * 2 + 2, g * 2 + 2, 0)
            attend(LAST, PAIRS - 1, 1, last=True)

        @block.sync
        def _(sp):
            def load_xt(b, t):
                sp.dma_start(xT[:, t, :, :, :].bitcast(F32), xt_s[b, :, t, :, :, :]).then_inc(xt_loaded[t], 16)

            def load_w1(e, i):
                sp.dma_start(w1t[:, i, :, :], w1[e, 0:C, :].rearrange("(k p) n -> p k n", p=P128)).then_inc(w1_loaded[i], 16)

            def load_w2(e, i):
                sp.dma_start(w2t[:, i, :, :, :].rearrange("p j c n -> p j (c n)"),
                             w2[e, 0:HID, :].rearrange("(j p c) n -> p j (c n)", p=P128, c=2)).then_inc(w2_loaded[i], 16)

            def load_b1(G):
                for j in range(4):
                    sp.dma_start(b1[32 * j:32 * j + B, :, :],
                                 w1[bass.ds(G * GE, GE), C, j * Q4:(j + 1) * Q4].unsqueeze(0).to_broadcast([B, GE, Q4])
                                 ).then_inc(b1_loaded, 16)

            def load_b2(G):
                sp.dma_start(b2[0:B, :, :], w2[bass.ds(G * GE, GE), HID, :].unsqueeze(0).to_broadcast([B, GE, C])
                             ).then_inc(b2_loaded, 16)

            def next_w(P, p):
                sp.wait_ge(w_scaled, (P + 1) * KT)
                load_weights(sp, wraw, wq, wk, wv, p, wraw_loaded)

            def next_xt(b, t):
                sp.wait_ge(proj_done, (b * PAIRS + PAIRS - 1) * NT + t + 1)
                load_xt(b + 1, t)

            def group_loads(G, p, final=False, after1=True, after2=True, tiles=False):
                def used(kind, k):
                    sp.wait_ge(slot_done, slot_count(G, final, kind, k))

                def take(*ts):
                    for t in ts if tiles else ():
                        next_xt(0, t)

                used("layer2", 0)
                load_w2(G * GE + 2, 0)
                take(0, 1)
                if after1:
                    used("layer1", 0)
                    load_w1((G + 1) * GE + 2, 0)
                take(2)
                used("layer2", 1)
                load_w2(G * GE + 3, 1)
                take(3)
                if after1:
                    used("layer1", 1)
                    load_w1((G + 1) * GE + 3, 1)
                take(4)
                next_w(G, p)
                used("layer2", 2)
                if after1:
                    load_w2((G + 1) * GE, 0)
                take(5)
                if after2:
                    used("layer1", 2)
                    load_w1((G + 2) * GE, 0)
                take(6, 7)
                if after2:
                    used("layer1", 3)
                    load_w1((G + 2) * GE + 1, 1)
                    sp.wait_ge(slot_read, slot_count(G, final, "layer1", 3))
                    load_b1(G + 2)
                used("layer2", 3)
                if after1:
                    load_w2((G + 1) * GE + 1, 1)
                sp.wait_ge(slot_read, slot_count(G, final, "layer2", 3))
                for j in range(4):
                    sp.dma_start(o_s[:, j, bass.ds(G * GE, GE), :], part[32 * j:32 * j + B, :, :]).then_inc(part_stored, 16)
                if after1:
                    load_b2(G + 1)

            load_w1(0, 0)
            load_b1(0)
            load_w1(1, 1)
            load_weights(sp, wraw, wq, wk, wv, 2, wraw_loaded)
            sp.wait_ge(slot_done, 1)
            load_w1(2, 0)
            load_b2(0)
            sp.wait_ge(slot_done, 2)
            load_w1(3, 1)
            load_w2(0, 0)
            load_w2(1, 1)
            sp.wait_ge(slot_done, 3)
            load_w1(GE, 0)
            sp.wait_ge(slot_done, 4)
            load_w1(GE + 1, 1)
            sp.wait_ge(slot_read, GE)
            load_b1(1)
            group_loads(0, 3)
            with sp.Fori(1, 5) as G:
                group_loads(G, G + 3)
            group_loads(5, 0)
            group_loads(6, 1, after2=False, tiles=True)
            sp.wait_ge(slot_done, slot_count(6, False, "layer1", 3))
            sp.dma_start(wo[:, :, :, :].bitcast(F32), wo_s).then_inc(wo_loaded, 16)
            group_loads(7, 2, final=True, after1=False, after2=False)
            with sp.Fori(1, B - 1) as b:
                with sp.Fori(0, PAIRS - 3) as p:
                    next_w(b * PAIRS + p, p + 3)
                next_w(b * PAIRS + PAIRS - 3, 0)
                for t in range(NT):
                    next_xt(b, t)
                next_w(b * PAIRS + PAIRS - 2, 1)
                next_w(b * PAIRS + PAIRS - 1, 2)
            with sp.Fori(0, PAIRS - 3) as p:
                next_w((B - 1) * PAIRS + p, p + 3)
            next_w((B - 1) * PAIRS + PAIRS - 3, 0)
            sp.wait_ge(part_stored, PAIRS * 64)

        @block.gpsimd
        def _(pool):

            def rotate(TI, u):
                pool.wait_ge(rope_done, TI + 1)
                cq = rc[:, u, 0:P128].rearrange("p (h d) -> p h d", h=2)
                sq = rs[:, u, 0:P128].rearrange("p (h d) -> p h d", h=2)
                ck = rc[:, u, P128:].rearrange("p (h d) -> p h d", h=2)
                sk = rs[:, u, P128:].rearrange("p (h d) -> p h d", h=2)
                pool.tensor_tensor(rk[:, u, :, :], ck, sk, ALU.add).then_inc(rk_done, 1)
                pool.tensor_tensor(rq[:, u, :, 0, :], cq, sq, ALU.add)
                pool.wait_ge(rk_done, TI + 1)
                pool.tensor_tensor(rq[:, u, :, 1, :], cq, sq, ALU.add)
                pool.tensor_copy(kk[:, u, :, 0, :], rk[:, u, :, :]).then_inc(kh_done, 1)
                pool.wait_ge(kh_done, TI + 1)
                pool.tensor_tensor(kk[:, u, :, 1, :], rk[:, u, :, :], kk[:, u, :, 0, :].bitcast(F32), ALU.subtract).then_inc(rot_done, 1)

            def prologue():
                for t in range(NT):
                    if t >= 2:
                        pool.wait_ge(stackT_done, t - 1)
                    rotate(t, t % 2)

            def input_and_bias(y, t):
                u = t % 2
                pool.wait_ge(x_loaded[u], (y * (NT // 2) + t // 2 + 1) * 16)
                if t >= 2:
                    pool.wait_ge(y_done, y * NT + t - 1)
                pool.tensor_tensor(xb[:, u, :], xin[:, u, :], bob[:, :], ALU.add).then_inc(xb_done, 1)

            def next_weights(P, par, t, first):
                k = (t - 1) % 2
                hi, lo = w[:, par, 0, k, :], w[:, par, 1, k, :]
                if t in (1, 2):
                    if t == 1:
                        pool.wait_ge(wraw_loaded, (P + 1) * 48)
                        pool.wait_ge(proj_done, (P + 1) * NT)
                        if not first:
                            pool.wait_ge(w_lo, P * KT)
                    pool.tensor_tensor(hi, wraw[:, k, :], wscale[:, :], ALU.mult)
                elif t in (3, 4):
                    pool.tensor_tensor(wscaled[:, k, :], wraw[:, k, :], wscale[:, :], ALU.mult).then_inc(w_scaled, 1)
                elif t in (5, 6):
                    pool.wait_ge(w_scaled, (P + 1) * KT)
                    pool.tensor_tensor(lo, wscaled[:, k, :], hi.bitcast(F32), ALU.subtract).then_inc(w_lo, 1)

            def attend(P, p, par, first=False, last=False, group=None, final=False, crossing=None, yb=None, late=False):
                for t in range(NT):
                    if yb is not None:
                        input_and_bias(yb, t)
                    if not last:
                        TI = (P + 1) * NT + t
                        pool.wait_ge(stackT_done, TI - 1)
                        rotate(TI, t % 2)
                        next_weights(P, par, t, first)

            def tail():
                for t in range(NT):
                    input_and_bias(B - 1, t)

            prologue()
            pairs(pool, attend)
            tail()

        @block.scalar
        def _(act):
            def exp(SI, i, h):
                s = (2 * i + h) % 2
                act.wait_ge(max_done, SI + 1)
                act.activation(Pr[:, s, 0:(i + 1) * P128], pS[s][:, 0:(i + 1) * P128], ACT.Exp, bias=nmax[:, s:s + 1],
                               accum_out=psum_row[:, i % 2, h:h + 1]).then_inc(exp_done, 1)

            def evac(P, i, h):
                for c in range(CH[i]):
                    n = chunk0(i, h) + c
                    lo, hi = c * BANK, min((c + 1) * BANK, (i + 1) * P128)
                    act.wait_ge(t_done, P * CHUNKS + n + 1)
                    act.activation(PT[:, i % 2, h, lo:hi], pT[n % 2][:, 0:hi - lo], ACT.Copy).then_inc(evac_done, 1)

            def stack(TI, t, par, bank):
                act.wait_ge(stackT_done, TI + 1)
                act.activation(KS[:, par, :, t * P128:(t + 1) * P128],
                               bank[:, 2 * P128:].rearrange("p (h n) -> p h n", h=2), ACT.Copy)
                act.activation(QH[:, :, t * P128:(t + 1) * P128],
                               bank[:, 0:2 * P128].rearrange("p (h n) -> p h n", h=2), ACT.Copy).then_inc(stack_hi, 1)

            def gelu(G):
                act.activation(g[:, :, :], g[:, :, :], ACT.Gelu).then_inc(g_done, 1)

            def prologue():
                for t in range(NT - 1):
                    stack(t, t, 0, first_stack(t))
                act.wait_ge(slot_read, GE)
                gelu(0)
                exp(0, 0, 0)

            def load_x(y, t):
                act.dma_start(xin[:, t % 2, :], x[y, t * P128:(t + 1) * P128, :]).then_inc(x_loaded[t % 2], 16)

            def start_output(y):
                for j in range(4):
                    act.dma_start(wsp[j * E:(j + 1) * E, :], wsp_s[y, :, :]).then_inc(moe_loaded, 16)
                act.dma_start(oe[:, :], o_s[y, :, :, :].rearrange("j e c -> (j e) c")).then_inc(moe_loaded, 16)
                load_x(y, 0)
                load_x(y, 1)

            def rounded(y, t):
                if t == NT - 1:
                    act.wait_ge(o_done, (y + 1) * PAIRS * NT)
                if t >= 2:
                    act.wait_ge(y_mm, y * NT + t - 1)
                act.activation(oh[:, t % 2, :, :], OT[:, :, t * P128:(t + 1) * P128], ACT.Copy).then_inc(oh_done, 1)

            def store(y, t):
                u = t % 2
                act.wait_ge(y_done, y * NT + t + 1)
                act.dma_start(out[y, t * P128:(t + 1) * P128, :], yt[:, u, :]).then_inc(y_stored[u], 16)
                if t + 2 < NT:
                    act.wait_ge(xb_done, y * NT + t + 1)
                    load_x(y, t + 2)

            def attend(P, p, par, first=False, last=False, group=None, final=False, crossing=None, yb=None, late=False):
                if late:
                    act.wait_ge(part_stored, PAIRS * 64)
                    start_output(yb)
                for i in range(NT):
                    if i == NT // 2 and last:
                        start_output(B - 1)
                    if i == NT // 2 and crossing is not None and group is None:
                        start_output(crossing)
                    if i == 0:
                        stack(P * NT + NT - 1, NT - 1, par, stack_bank(0))
                    exp(P * STEPS + 2 * i + 1, i, 1)
                    if not first or i >= 2:
                        act.wait_ge(pv_done, P * NT + i - 1)
                    evac(P, i, 0)
                    if yb is not None:
                        for t in (0, 1) if i == 0 else range(i + 1, min(i + 2, NT)):
                            rounded(yb, t)
                    if i > 0 and not last:
                        stack((P + 1) * NT + i - 1, i - 1, 1 - par, stack_bank(i))
                    if i + 1 < NT:
                        exp(P * STEPS + 2 * i + 2, i + 1, 0)
                    elif not last:
                        exp(P * STEPS + STEPS, 0, 0)
                    evac(P, i, 1)
                    if yb is not None and i > 0:
                        store(yb, i - 1)
                if yb is not None:
                    store(yb, NT - 1)
                if group is not None and not final:
                    act.wait_ge(slot_read, slot_count(group, False, "layer1", 3))
                    gelu(group + 1)

            def tail():
                act.wait_ge(o_done, B * PAIRS * NT - 1)
                rounded(B - 1, 0)
                rounded(B - 1, 1)
                for t in range(NT):
                    if t + 2 < NT:
                        rounded(B - 1, t + 2)
                    store(B - 1, t)

            prologue()
            pairs(act, attend)
            tail()
            for u in range(2):
                act.wait_ge(y_stored[u], B * NT // 2 * 16)

        @block.vector
        def _(dve):
            def rope(TI, t, par, bank):
                u = t % 2
                dve.wait_ge(proj_done, TI + 1)
                q2 = bank[:, 0:2 * P128]
                four = [P128, 4, DH]
                dve.tensor_tensor(rc[:, u, :].rearrange("p (g d) -> p g d", d=DH), q2.rearrange("p (g d) -> p g d", d=DH),
                                  cos[:, t, :].unsqueeze(1).to_broadcast(four), ALU.mult)
                for o in range(2):
                    dve.tensor_tensor(rs[:, u, :].rearrange("p (g d o) -> p g d o", d=DH // 2, o=2)[:, :, :, o],
                                      q2.rearrange("p (g d o) -> p g d o", d=DH // 2, o=2)[:, :, :, 1 - o],
                                      sin[:, t, o::2].unsqueeze(1).to_broadcast([P128, 4, DH // 2]), ALU.mult)
                dve.tensor_copy(V[:, par, t, :], bank[:, 2 * P128:QKV]).then_inc(rope_done, 1)

            def stack(TI, t, par, bank):
                dve.wait_ge(stack_hi, TI + 1)
                dve.tensor_tensor(QL[:, :, t * P128:(t + 1) * P128], bank[:, 0:2 * P128].rearrange("p (h n) -> p h n", h=2),
                                  QH[:, :, t * P128:(t + 1) * P128].bitcast(F32), ALU.subtract).then_inc(stack_lo, 1)

            def row_max(SI, i, h):
                s = (2 * i + h) % 2
                dve.wait_ge(s_done, SI + 1)
                dve.tensor_reduce(nmax[:, s:s + 1], pS[s][:, 0:(i + 1) * P128], AX_X, ALU.max, negate=True).then_inc(max_done, 1)

            def reciprocals(OI, SI, i):
                dve.wait_ge(exp_done, SI + 1)
                dve.reciprocal(recip[:, i % 2, :], psum_row[:, i % 2, :]).then_inc(recip_done, 1)

            def replicate(OI, i):
                dve.wait_ge(recip_done, OI + 1)
                dve.tensor_scalar(rep[:, i % 2, :, :], recip[:, i % 2, :].unsqueeze(2).to_broadcast([P128, 2, DH]),
                                  1.0, None, ALU.mult).then_inc(rep_done, 1)

            def values(OI, p, i):
                dve.wait_ge(pv_done, OI + 1)
                dve.tensor_copy(rT[:, :], pO[:, P128:2 * P128]).then_inc(rt_copied, 1)
                dve.wait_ge(rt_copied, OI + 1)
                dve.tensor_tensor(OT[:, p, i * P128:(i + 1) * P128], pO[:, 0:P128], rT[:, :], ALU.mult).then_inc(o_done, 1)

            def merged(G):
                for k in range(GE):
                    copy = dve.tensor_copy(mT[:, k, :, 0:B], mgT[:, :, :, G * GE + k])
                copy.then_inc(mT_done, 1)

            def read_slot(G, kind, k, n, bank, more=True):
                dve.wait_ge(slot_done, n + 1)
                if kind == "layer1":
                    if k == 0:
                        dve.wait_ge(b1_loaded, (G + 1) * 64)
                    dve.tensor_tensor(g[:, k, :], bank, b1[:, k, :], ALU.add).then_inc(slot_read, 1)
                elif kind == "turn":
                    dve.tensor_copy(hT[:, :, :].rearrange("p c m -> p (c m)"), bank).then_inc(slot_read, 1)
                else:
                    if k == 0:
                        dve.wait_ge(b2_loaded, (G + 1) * 16)
                        if more:
                            dve.wait_ge(part_stored, G * 64)
                    dve.tensor_tensor(part[:, k, :], bank, b2[:, k, :], ALU.add).then_inc(slot_read, 1)

            def read_slots(G, final, i, before, first):
                for kind, k, n in slots_at(G, final, i, before):
                    read_slot(G + 1 if kind == "layer1" else G, kind, k, n, pO[:, 2 * P128:], more=not first)
                    if kind == "layer1" and k == GE - 1:
                        merged(G + 2)

            def prologue():
                merged(0)
                for t in range(NT):
                    if t >= 2:
                        dve.wait_ge(rot_done, t - 1)
                    rope(t, t, 0, first_bank(t))
                    if t % 2 == 1:
                        read_slot(0, "layer1", t // 2, t // 2, pT[t // 2 % 2][:, 0:Q4])
                    if t >= 2:
                        stack(t - 2, t - 2, 0, first_stack(t - 2))
                stack(NT - 2, NT - 2, 0, first_stack(NT - 2))
                merged(1)
                row_max(0, 0, 0)

            def rest(y, t):
                dve.wait_ge(oh_done, y * NT + t + 1)
                if t >= 2:
                    dve.wait_ge(y_mm, y * NT + t - 1)
                dve.tensor_tensor(ol[:, t % 2, :, :], OT[:, :, t * P128:(t + 1) * P128], oh[:, t % 2, :, :].bitcast(F32),
                                  ALU.subtract).then_inc(ol_done, 1)

            def output(y, t, bank):
                u = t % 2
                dve.wait_ge(y_mm, y * NT + t + 1)
                dve.wait_ge(xb_done, y * NT + t + 1)
                dve.wait_ge(y_stored[u], (y * (NT // 2) + t // 2) * 16)
                dve.tensor_tensor(yt[:, u, :], bank, xb[:, u, :], ALU.add).then_inc(y_done, 1)

            def attend(P, p, par, first=False, last=False, group=None, final=False, crossing=None, yb=None, late=False):
                for i in range(NT):
                    if i > 0:
                        read_slots(group, final, i - 1, False, first)
                        reciprocals(P * NT + i - 1, P * STEPS + 2 * i - 1, i - 1)
                    elif not first:
                        reciprocals(P * NT - 1, P * STEPS - 1, NT - 1)
                    row_max(P * STEPS + 2 * i + 1, i, 1)
                    if i > 0:
                        replicate(P * NT + i - 1, i - 1)
                    elif not first:
                        replicate(P * NT - 1, NT - 1)
                    read_slots(group, final, i, True, first)
                    if yb is not None and i > 0:
                        output(yb, i - 1, pO[:, 2 * P128:])
                    if i == 0:
                        stack(P * NT + NT - 1, NT - 1, par, stack_bank(0))
                    if i == 0 and not first:
                        values(P * NT - 1, PAIRS - 1 if yb is not None else p - 1, NT - 1)
                    if not last:
                        if not first or i >= 2:
                            dve.wait_ge(rot_done, (P + 1) * NT + i - 1)
                        rope((P + 1) * NT + i, i, 1 - par, pP)
                    if i > 0:
                        values(P * NT + i - 1, p, i - 1)
                    if yb is not None:
                        for t in (0, 1) if i == 0 else range(i + 1, min(i + 2, NT)):
                            rest(yb, t)
                    if i + 1 < NT:
                        row_max(P * STEPS + 2 * i + 2, i + 1, 0)
                    elif not last:
                        row_max(P * STEPS + STEPS, 0, 0)
                    if i > 0 and not last:
                        stack((P + 1) * NT + i - 1, i - 1, 1 - par, stack_bank(i))
                if yb is not None:
                    output(yb, NT - 1, pO[:, 2 * P128:])
                read_slots(group, final, NT - 1, False, first)

            def tail():
                reciprocals(LAST * NT + NT - 1, LAST * STEPS + STEPS - 1, NT - 1)
                replicate(LAST * NT + NT - 1, NT - 1)
                rest(B - 1, 0)
                rest(B - 1, 1)
                values(LAST * NT + NT - 1, PAIRS - 1, NT - 1)
                for t in range(NT):
                    output(B - 1, t, pT[t % 2][:, 0:C])
                    if t + 2 < NT:
                        rest(B - 1, t + 2)

            prologue()
            pairs(dve, attend)
            tail()

        @block.tensor
        def _(pe):

            def project(TI, t, par, bank):
                n = 0
                for k in range(KT):
                    for hx, hw in ((0, 0), (0, 1), (1, 0)):
                        mm = pe.matmul(bank[:, 0:QKV], xT[:, t, hx, k, :], w[:, par, hw, k, :],
                                       start=(n == 0), stop=(n == 3 * KT - 1))
                        n += 1
                mm.then_inc(proj_done, 1)

            def stack(TI, t, bank):
                u = t % 2
                pe.wait_ge(rot_done, TI + 1)
                for h in range(2):
                    pe.transpose(bank[:, h * P128:(h + 1) * P128], rq[:, u, h, :, :].rearrange("p a d -> p (a d)"), ident[:, :])
                for h in range(2):
                    mm = pe.matmul(bank[:, (2 + h) * P128:(3 + h) * P128], kk[:, u, h, :, :].rearrange("p a d -> p (a d)"),
                                   identr[:, :], start=True, stop=True)
                mm.then_inc(stackT_done, 1)

            def scores(TI, SI, i, h, par, fresh):
                s = (2 * i + h) % 2
                pe.wait_ge(stack_lo, TI + 1)
                if not fresh:
                    pe.wait_ge(exp_done, SI - 1)
                width = (i + 1) * P128
                q = slice(i * P128, (i + 1) * P128)
                for c0 in range(0, width, BANK):
                    c1 = min(c0 + BANK, width)
                    diag = c1 == width
                    pe.matmul(pS[s][:, c0:c1], QH[:, h, q], KS[:, par, h, c0:c1], start=True, stop=False)
                    mm = pe.matmul(pS[s][:, c0:c1], QL[:, h, q], KS[:, par, h, c0:c1], start=False, stop=not diag)
                mm = pe.matmul(pS[s][:, width - P128:width], identb[:, :], maskb[:, :], start=False, stop=True)
                mm.then_inc(s_done, 1)

            def transposes(P, SI, i, h, lag):
                s = (2 * i + h) % 2
                pe.wait_ge(exp_done, SI + 1)
                for c in range(CH[i]):
                    n = chunk0(i, h) + c
                    if lag or n >= 2:
                        pe.wait_ge(evac_done, P * CHUNKS + n - 1)
                    for j in range(4 * c, min(4 * c + 4, i + 1)):
                        tr = pe.transpose(pT[n % 2][:, (j - 4 * c) * P128:(j - 4 * c + 1) * P128],
                                          Pr[:, s, j * P128:(j + 1) * P128], ident[:, :])
                    tr.then_inc(t_done, 1)

            def values(P, OI, i, par):
                pe.wait_ge(rep_done, OI + 1)
                pe.wait_ge(o_done, OI)
                pe.transpose(pO[:, P128:2 * P128], rep[:, i % 2, :, :].rearrange("p h d -> p (h d)"), ident[:, :])
                pe.wait_ge(evac_done, P * CHUNKS + chunk0(i, 1) + CH[i])
                for j in range(i + 1):
                    for h in range(2):
                        mm = pe.matmul(pO[h * DH:(h + 1) * DH, 0:P128], V[:, par, j, h * DH:(h + 1) * DH],
                                       PT[:, i % 2, h, j * P128:(j + 1) * P128], start=(j == 0), stop=(j == i))
                mm.then_inc(pv_done, 1)

            def slot(G, kind, k, n, bank, first=False):
                if not first:
                    pe.wait_ge(slot_read, n)
                if kind == "layer1":
                    pe.wait_ge(mT_done, G + 1)
                    pe.wait_ge(w1_loaded[k % 2], (G * (GE // 2) + k // 2 + 1) * 16)
                    for c in range(KT):
                        for j in range(4):
                            mm = pe.matmul(bank[32 * j:32 * j + 32, :], mT[:, k, c, :], w1t[:, k % 2, c, j * Q4:(j + 1) * Q4],
                                           start=(c == 0), stop=(c == KT - 1))
                elif kind == "turn":
                    pe.wait_ge(g_done, G + 1)
                    for c in range(2):
                        mm = pe.transpose(bank[:, c * P128:(c + 1) * P128], g[:, k, c::2], ident[:, :])
                else:
                    pe.wait_ge(w2_loaded[k % 2], (G * (GE // 2) + k // 2 + 1) * 16)
                    for c in range(2):
                        for j in range(4):
                            mm = pe.matmul(bank[32 * j:32 * j + 32, :], hT[:, c, 32 * j:32 * j + 32], w2t[:, k % 2, j, c, :],
                                           start=(c == 0), stop=(c == 1))
                mm.then_inc(slot_done, 1)

            def slots(G, final, i, before, o_count, fresh=False):
                for kind, k, n in slots_at(G, final, i, before):
                    if not fresh:
                        pe.wait_ge(o_done, o_count)
                    slot(G + 1 if kind == "layer1" else G, kind, k, n, pO[:, 2 * P128:])

            def slots_over(G, final, i):
                if G is not None:
                    pe.wait_ge(slot_read, [n for s, n in slots_of(G, final) if s[0] < i or s[:2] == (i, True)][-1] + 1)

            def output(y, t, bank):
                u = t % 2
                pe.matmul(bank, wsp[:, t * P128:(t + 1) * P128], oe[:, :], start=True, stop=False)
                pe.wait_ge(ol_done, y * NT + t + 1)
                n = 0
                for k in range(PAIRS):
                    for o, hw in ((oh, 0), (oh, 1), (ol, 0)):
                        n += 1
                        mm = pe.matmul(bank, o[:, u, k, :], wo[:, hw, k, :], start=False, stop=(n == 3 * PAIRS))
                mm.then_inc(y_mm, 1)

            def prologue():
                for t in range(NT):
                    if t >= 4:
                        pe.wait_ge(rope_done, t - 3)
                    project(t, t, 0, first_bank(t))
                    if t >= 2:
                        if t >= 4:
                            pe.wait_ge(stack_lo, t - 3)
                        stack(t - 2, t - 2, first_stack(t - 2))
                    if t % 2 == 1:
                        slot(0, "layer1", t // 2, t // 2, pT[t // 2 % 2][:, 0:Q4], first=(t == 1))
                pe.wait_ge(stack_lo, NT - 3)
                stack(NT - 2, NT - 2, first_stack(NT - 2))
                pe.wait_ge(rope_done, NT)
                scores(0, 0, 0, 0, 0, True)
                pe.wait_ge(slot_read, GE)

            def attend(P, p, par, first=False, last=False, group=None, final=False, crossing=None, yb=None, late=False):
                if not last and not first:
                    pe.wait_ge(w_lo, P * KT)
                for i in range(NT):
                    SI = P * STEPS + 2 * i
                    scores(P * NT + i, SI + 1, i, 1, par, first and i == 0)
                    TI = (P + 1) * NT + i
                    if i == 0:
                        stack(P * NT + NT - 1, NT - 1, stack_bank(i))
                        transposes(P, SI, i, 0, not first)
                        if not first:
                            if group is not None:
                                pe.wait_ge(slot_read, slots_of(group, False)[0][1])
                            elif yb is not None:
                                pe.wait_ge(slot_read, slot_count(PAIRS - 1, True, "layer2", GE - 1))
                            values(P - 1, P * NT - 1, NT - 1, 1 - par)
                    if not last:
                        if crossing is not None:
                            pe.wait_ge(xt_loaded[i], (crossing + 1) * 16)
                        if i in (1, 2, 3):
                            pe.wait_ge(rope_done, TI)
                        else:
                            pe.wait_ge(stack_lo, TI - 1)
                        project(TI, i, 1 - par, pP)
                    if i > 0:
                        slots(group, final, i, True, P * NT + i - 1)
                        transposes(P, SI, i, 0, True)
                        slots_over(group, final, i)
                        if yb is not None:
                            pe.wait_ge(y_done, yb * NT + i)
                        values(P, P * NT + i - 1, i - 1, par)
                    if i + 1 < NT:
                        scores(P * NT + i + 1, SI + 2, i + 1, 0, par, False)
                    elif not last:
                        scores((P + 1) * NT, SI + 2, 0, 0, 1 - par, False)
                    if i > 0 and not last:
                        if i < 3:
                            pe.wait_ge(stack_lo, (P + 1) * NT + i - 1)
                        else:
                            pe.wait_ge(rope_done, (P + 1) * NT + i + 1)
                        stack((P + 1) * NT + i - 1, i - 1, stack_bank(i))
                    transposes(P, SI + 1, i, 1, not first)
                    slots(group, final, i, False, P * NT + i, fresh=(first and i == 0))
                    if yb is not None:
                        if i == 0:
                            pe.wait_ge(wo_loaded, 16)
                            pe.wait_ge(moe_loaded, (yb + 1) * 80)
                        pe.wait_ge(o_done, P * NT + i)
                        output(yb, i, pO[:, 2 * P128:])
                if yb is not None:
                    pe.wait_ge(y_done, (yb + 1) * NT)

            def tail():
                values(LAST, LAST * NT + NT - 1, NT - 1, 1)
                pe.wait_ge(moe_loaded, B * 80)
                pe.wait_ge(evac_done, B * PAIRS * CHUNKS)
                for t in range(NT):
                    if t >= 2:
                        pe.wait_ge(y_done, (B - 1) * NT + t - 1)
                    output(B - 1, t, pT[t % 2][:, 0:C])

            prologue()
            pairs(pe, attend)
            tail()


def build(nc, x, wq, wk, wv, wo, bo, gate_w, gate_b, w1, w2, rot_cos, rot_sin, out):
    def dram(name, shape):
        return nc.dram_tensor(name, shape, F32, kind="Internal").ap()

    xt_s = dram("xt_s", (B, P128, NT, 2, KT, P128))
    wo_s = dram("wo_s", (P128, 2, PAIRS, C))
    wsp_s = dram("wsp_s", (B, E, T))
    o_s = dram("o_s", (B, 4, E, C))
    with ExitStack() as ctx:
        def sb(name, shape, dt=F32):
            return ctx.enter_context(nc.sbuf_tensor(name, shape, dt))

        mgT = sb("s_mgT", [P128, KT, B, E + GE])
        xT = sb("s_xT", [P128, NT, 2, KT, P128], F32R)
        w = sb("s_w", [P128, 2, 2, KT, QKV], F32R)
        wraw = sb("s_wraw", [P128, KT, QKV])
        wscaled = sb("s_wscaled", [P128, KT, QKV])
        wscale = sb("s_wscale", [P128, QKV])
        mT = sb("s_mT", [P128, GE, KT, 32])
        b1 = sb("s_b1", [P128, GE, Q4])
        b2 = sb("s_b2", [P128, GE, C])
        bob = sb("s_bob", [P128, C])
        cos = sb("s_cos", [P128, NT, DH])
        sin = sb("s_sin", [P128, NT, DH])
        ident = sb("s_ident", [P128, P128])
        identr = sb("s_identr", [P128, P128], F32R)
        identb = sb("s_identb", [P128, P128], BF16)
        maskb = sb("s_maskb", [P128, P128], BF16)
        consts = (ident, identr, identb, maskb)
        with nc.sbuf_tensor("s_xn", [P128, B, NT, C], F32) as xn, nc.sbuf_tensor("s_L", [P128, T], F32) as L, \
                nc.sbuf_tensor("s_woraw", [P128, PAIRS, C], F32) as woraw:
            prepare_block(nc, x, gate_w, gate_b, wq, wk, wv, wo, woraw, xt_s, L, xn, w, wraw, wscaled, wscale, consts)
            route_block(nc, woraw, rot_cos, rot_sin, L, xt_s, wsp_s, wo_s, xn, mgT, xT, cos, sin, ident,
                        bo, mT, b1, b2, bob)
        attend_block(nc, x, wq, wk, wv, w1, w2, xt_s, wo_s, wsp_s, o_s, mgT, xT, w, wraw, wscaled, wscale,
                     cos, sin, consts, mT, b1, b2, bob, out)


_INS = ["L0_attn_x", "L0_attn_Wq", "L0_attn_Wk", "L0_attn_Wv", "L0_attn_Wo", "L0_attn_bo",
        "L0_ffn_gate_w", "L0_ffn_gate_b", "L0_ffn_w1", "L0_ffn_w2"]


def rotation_tables():
    import numpy as np
    inv = (1.0 / 10000.0 ** (np.arange(0, DH, 2, dtype=np.float32) / np.float32(DH))).astype(np.float32)
    ang = (np.arange(T, dtype=np.float32)[:, None] * inv[None, :]).astype(np.float32)
    cos = np.repeat(np.cos(ang), 2, axis=1)
    sin = np.stack([-np.sin(ang), np.sin(ang)], axis=-1).reshape(T, DH)
    return np.ascontiguousarray(cos, dtype=np.float32), np.ascontiguousarray(sin, dtype=np.float32)


def kernel(**inputs):
    import numpy as _np
    import concourse.bacc as _bacc
    from concourse import mybir as _mybir
    from concourse.bass_utils import run_bass_kernel_spmd as _run

    nc = _bacc.Bacc("TRN2", target_bir_lowering=False, num_devices=1)
    cos, sin = rotation_tables()
    arrays, args = {}, []
    for name, a in [(n, inputs[n]) for n in _INS] + [("rot_cos", cos), ("rot_sin", sin)]:
        a = _np.ascontiguousarray(a)
        arrays[f"in_{name}"] = a
        args.append(nc.dram_tensor(f"in_{name}", a.shape, _mybir.dt.from_np(a.dtype), kind="ExternalInput").ap())
    args.append(nc.dram_tensor("out_0", (B, T, C), F32, kind="ExternalOutput").ap())
    build(nc, *args)
    r = _run(nc, [arrays], core_ids=[0])
    return r.results[0]["out_0"]
```
